# Optimizing a Trainium2 kernel written in Bass

```python
import numpy as np
import jax
import jax.numpy as jnp

def _softmax(x, axis=-1):
    return jax.nn.softmax(x, axis=axis)

def _gelu(x):
    return jax.nn.gelu(x, approximate=True)

def _silu(x):
    return jax.nn.silu(x)

def _sigmoid(x):
    return jax.nn.sigmoid(x)

def _layernorm(x, axis=-1, eps=1e-05):
    m = jnp.mean(x, axis=axis, keepdims=True)
    v = jnp.var(x, axis=axis, keepdims=True)
    return (x - m) / jnp.sqrt(v + eps)

def _scatter_add(tgt, idx, src, axis=0):
    return tgt.at[idx].add(src)

def _segment_sum(src, seg, n):
    return jax.ops.segment_sum(src, seg, n)
kernel_name = 'mk_adaln_d1_jaxref_r8_ef8d47'

def setup_inputs(seed: int=0):
    np.random.seed(seed)
    _w = jnp.asarray

    def _L0_attn_setup():
        import jax, jax.numpy as jnp
        import numpy as np
        D_MODEL, D_STATE, D_CONV, EXPAND = (128, 16, 4, 2)
        D_INNER = EXPAND * D_MODEL
        DT_RANK = (D_MODEL + 15) // 16
        B_SZ, SEQ = (2, 128)

        def _mamba_dir(x, inW, convW, convB, xpW, dtW, dtB, Alog, Dp, outW):
            Bsz, L, _ = x.shape
            d_inner, d_state = Alog.shape
            dt_rank = xpW.shape[0] - 2 * d_state
            xz = jnp.einsum('bld,ed->ble', x, inW)
            xi, z = jnp.split(xz, 2, axis=-1)
            xc = jnp.swapaxes(xi, 1, 2)
            xc = jax.lax.conv_general_dilated(xc, convW, window_strides=(1,), padding=[(convW.shape[-1] - 1, 0)], feature_group_count=d_inner)
            xc = xc + convB[None, :, None]
            u = jax.nn.silu(jnp.swapaxes(xc, 1, 2))
            x_dbl = jnp.einsum('bld,ed->ble', u, xpW)
            dt, Bm, Cm = jnp.split(x_dbl, [dt_rank, dt_rank + d_state], axis=-1)
            delta = jax.nn.softplus(jnp.einsum('blr,dr->bld', dt, dtW) + dtB)
            A = -jnp.exp(Alog)

            def step(h, ins):
                d_t, B_t, C_t, u_t = ins
                dA = jnp.exp(d_t[:, :, None] * A)
                h = h * dA + (d_t * u_t)[:, :, None] * B_t[:, None, :]
                y_t = jnp.einsum('bdn,bn->bd', h, C_t)
                return (h, y_t)
            h0 = jnp.zeros((Bsz, d_inner, d_state), x.dtype)
            xs = (jnp.swapaxes(delta, 0, 1), jnp.swapaxes(Bm, 0, 1), jnp.swapaxes(Cm, 0, 1), jnp.swapaxes(u, 0, 1))
            _, ys = jax.lax.scan(step, h0, xs)
            y = jnp.swapaxes(ys, 0, 1)
            y = y + u * Dp
            y = y * jax.nn.silu(z)
            return jnp.einsum('bld,od->blo', y, outW)

        def _make_params(key, suffix):
            ks = jax.random.split(key, 10)
            s = 0.02
            p = {'inW' + suffix: jax.random.normal(ks[0], (2 * D_INNER, D_MODEL), jnp.float32) * s, 'convW' + suffix: jax.random.normal(ks[1], (D_INNER, 1, D_CONV), jnp.float32) * s, 'convB' + suffix: jnp.zeros((D_INNER,), jnp.float32), 'xpW' + suffix: jax.random.normal(ks[2], (DT_RANK + 2 * D_STATE, D_INNER), jnp.float32) * s, 'dtW' + suffix: jax.random.normal(ks[3], (D_INNER, DT_RANK), jnp.float32) * s, 'dtB' + suffix: jax.random.normal(ks[4], (D_INNER,), jnp.float32) * 0.1 - 4.0, 'Alog' + suffix: jnp.log(1.0 + jax.random.uniform(ks[5], (D_INNER, D_STATE), jnp.float32) * 15.0), 'Dp' + suffix: jnp.ones((D_INNER,), jnp.float32), 'outW' + suffix: jax.random.normal(ks[6], (D_MODEL, D_INNER), jnp.float32) * s}
            return p
        key = jax.random.key(seed)
        kx, kf, kb = jax.random.split(key, 3)
        inp = {'x': jax.random.normal(kx, (B_SZ, SEQ, D_MODEL), jnp.float32)}
        inp.update(_make_params(kf, '_f'))
        inp.update(_make_params(kb, '_b'))
        return inp
    _L0_attn_in = _L0_attn_setup()

    def _L0_ffn_setup():
        import jax, jax.numpy as jnp
        import numpy as np
        HIDDEN = 128
        NUM_EXPERTS = 8
        TOP_K = 2
        key = jax.random.key(seed)
        k_x, k_r, k_w1, k_w2 = jax.random.split(key, 4)
        x = jax.random.normal(k_x, (4, 256, HIDDEN), dtype=jnp.float32)
        router_w = jax.random.normal(k_r, (NUM_EXPERTS, HIDDEN), dtype=jnp.float32) * HIDDEN ** (-0.5)
        w1 = jax.random.normal(k_w1, (NUM_EXPERTS, HIDDEN, 2 * HIDDEN), dtype=jnp.float32) * HIDDEN ** (-0.5)
        w2 = jax.random.normal(k_w2, (NUM_EXPERTS, 2 * HIDDEN, HIDDEN), dtype=jnp.float32) * (2 * HIDDEN) ** (-0.5)
        return {'x': x, 'router_w': router_w, 'w1': w1, 'w2': w2}
    _L0_ffn_in = _L0_ffn_setup()
    _L0_c = _w((lambda *s: np.random.randn(*s).astype(np.float32) * 0.05)(16, 128))
    _L0_wmod = _w((lambda *s: np.random.randn(*s).astype(np.float32) * 0.05)(128, 6 * 128) * 128 ** (-0.5))
    _d = {'L0_attn_x': _L0_attn_in['x'], 'L0_attn_inW_f': _L0_attn_in['inW_f'], 'L0_attn_convW_f': _L0_attn_in['convW_f'], 'L0_attn_convB_f': _L0_attn_in['convB_f'], 'L0_attn_xpW_f': _L0_attn_in['xpW_f'], 'L0_attn_dtW_f': _L0_attn_in['dtW_f'], 'L0_attn_dtB_f': _L0_attn_in['dtB_f'], 'L0_attn_Alog_f': _L0_attn_in['Alog_f'], 'L0_attn_Dp_f': _L0_attn_in['Dp_f'], 'L0_attn_outW_f': _L0_attn_in['outW_f'], 'L0_attn_inW_b': _L0_attn_in['inW_b'], 'L0_attn_convW_b': _L0_attn_in['convW_b'], 'L0_attn_convB_b': _L0_attn_in['convB_b'], 'L0_attn_xpW_b': _L0_attn_in['xpW_b'], 'L0_attn_dtW_b': _L0_attn_in['dtW_b'], 'L0_attn_dtB_b': _L0_attn_in['dtB_b'], 'L0_attn_Alog_b': _L0_attn_in['Alog_b'], 'L0_attn_Dp_b': _L0_attn_in['Dp_b'], 'L0_attn_outW_b': _L0_attn_in['outW_b'], 'L0_ffn_router_w': _L0_ffn_in['router_w'], 'L0_ffn_w1': _L0_ffn_in['w1'], 'L0_ffn_w2': _L0_ffn_in['w2'], 'L0_c': _L0_c, 'L0_wmod': _L0_wmod}
    _x0 = _d['L0_attn_x']
    _d['L0_attn_x'] = jax.random.normal(jax.random.fold_in(jax.random.key(seed), 1), (16, 256, 128), dtype=_x0.dtype)
    del _x0
    return _d

def reference(L0_attn_x, L0_attn_inW_f, L0_attn_convW_f, L0_attn_convB_f, L0_attn_xpW_f, L0_attn_dtW_f, L0_attn_dtB_f, L0_attn_Alog_f, L0_attn_Dp_f, L0_attn_outW_f, L0_attn_inW_b, L0_attn_convW_b, L0_attn_convB_b, L0_attn_xpW_b, L0_attn_dtW_b, L0_attn_dtB_b, L0_attn_Alog_b, L0_attn_Dp_b, L0_attn_outW_b, L0_ffn_router_w, L0_ffn_w1, L0_ffn_w2, L0_c, L0_wmod):

    def _L0_attn_ref(x, inW_f, convW_f, convB_f, xpW_f, dtW_f, dtB_f, Alog_f, Dp_f, outW_f, inW_b, convW_b, convB_b, xpW_b, dtW_b, dtB_b, Alog_b, Dp_b, outW_b):
        import jax, jax.numpy as jnp
        import numpy as np
        D_MODEL, D_STATE, D_CONV, EXPAND = (128, 16, 4, 2)
        D_INNER = EXPAND * D_MODEL
        DT_RANK = (D_MODEL + 15) // 16
        B_SZ, SEQ = (2, 128)

        def _mamba_dir(x, inW, convW, convB, xpW, dtW, dtB, Alog, Dp, outW):
            Bsz, L, _ = x.shape
            d_inner, d_state = Alog.shape
            dt_rank = xpW.shape[0] - 2 * d_state
            xz = jnp.einsum('bld,ed->ble', x, inW)
            xi, z = jnp.split(xz, 2, axis=-1)
            xc = jnp.swapaxes(xi, 1, 2)
            xc = jax.lax.conv_general_dilated(xc, convW, window_strides=(1,), padding=[(convW.shape[-1] - 1, 0)], feature_group_count=d_inner)
            xc = xc + convB[None, :, None]
            u = jax.nn.silu(jnp.swapaxes(xc, 1, 2))
            x_dbl = jnp.einsum('bld,ed->ble', u, xpW)
            dt, Bm, Cm = jnp.split(x_dbl, [dt_rank, dt_rank + d_state], axis=-1)
            delta = jax.nn.softplus(jnp.einsum('blr,dr->bld', dt, dtW) + dtB)
            A = -jnp.exp(Alog)

            def step(h, ins):
                d_t, B_t, C_t, u_t = ins
                dA = jnp.exp(d_t[:, :, None] * A)
                h = h * dA + (d_t * u_t)[:, :, None] * B_t[:, None, :]
                y_t = jnp.einsum('bdn,bn->bd', h, C_t)
                return (h, y_t)
            h0 = jnp.zeros((Bsz, d_inner, d_state), x.dtype)
            xs = (jnp.swapaxes(delta, 0, 1), jnp.swapaxes(Bm, 0, 1), jnp.swapaxes(Cm, 0, 1), jnp.swapaxes(u, 0, 1))
            _, ys = jax.lax.scan(step, h0, xs)
            y = jnp.swapaxes(ys, 0, 1)
            y = y + u * Dp
            y = y * jax.nn.silu(z)
            return jnp.einsum('bld,od->blo', y, outW)

        def _make_params(key, suffix):
            ks = jax.random.split(key, 10)
            s = 0.02
            p = {'inW' + suffix: jax.random.normal(ks[0], (2 * D_INNER, D_MODEL), jnp.float32) * s, 'convW' + suffix: jax.random.normal(ks[1], (D_INNER, 1, D_CONV), jnp.float32) * s, 'convB' + suffix: jnp.zeros((D_INNER,), jnp.float32), 'xpW' + suffix: jax.random.normal(ks[2], (DT_RANK + 2 * D_STATE, D_INNER), jnp.float32) * s, 'dtW' + suffix: jax.random.normal(ks[3], (D_INNER, DT_RANK), jnp.float32) * s, 'dtB' + suffix: jax.random.normal(ks[4], (D_INNER,), jnp.float32) * 0.1 - 4.0, 'Alog' + suffix: jnp.log(1.0 + jax.random.uniform(ks[5], (D_INNER, D_STATE), jnp.float32) * 15.0), 'Dp' + suffix: jnp.ones((D_INNER,), jnp.float32), 'outW' + suffix: jax.random.normal(ks[6], (D_MODEL, D_INNER), jnp.float32) * s}
            return p
        y_fwd = _mamba_dir(x, inW_f, convW_f, convB_f, xpW_f, dtW_f, dtB_f, Alog_f, Dp_f, outW_f)
        xb = jnp.flip(x, axis=1)
        y_bwd = jnp.flip(_mamba_dir(xb, inW_b, convW_b, convB_b, xpW_b, dtW_b, dtB_b, Alog_b, Dp_b, outW_b), axis=1)
        return 0.5 * (y_fwd + y_bwd)

    def _L0_ffn_ref(x, router_w, w1, w2):
        import jax, jax.numpy as jnp
        import numpy as np
        HIDDEN = 128
        NUM_EXPERTS = 8
        TOP_K = 2
        bsz, seq, hidden = x.shape
        tokens = x.reshape(-1, hidden)
        logits = tokens @ router_w.T
        topk_vals, topk_idx = jax.lax.top_k(logits, TOP_K)
        weights = jax.nn.softmax(topk_vals, axis=-1)
        h = jnp.einsum('td,edf->etf', tokens, w1)
        h = jax.nn.gelu(h, approximate=False)
        out_all = jnp.einsum('etf,efd->etd', h, w2)
        out_ted = jnp.transpose(out_all, (1, 0, 2))
        gathered = jnp.take_along_axis(out_ted, topk_idx[:, :, None], axis=1)
        output = jnp.sum(weights[:, :, None] * gathered, axis=1)
        return output.reshape(bsz, seq, hidden)
    x = L0_attn_x
    mod = (_silu(L0_c) @ L0_wmod).reshape(L0_c.shape[0], 6, 1, -1)
    sa, ca, ga, sb, cb, gb = (mod[:, 0], mod[:, 1], mod[:, 2], mod[:, 3], mod[:, 4], mod[:, 5])
    ga = (2 * (ga >= 0) - 1) * jnp.maximum(jnp.abs(ga), 0.25)
    gb = (2 * (gb >= 0) - 1) * jnp.maximum(jnp.abs(gb), 0.25)
    h = _layernorm(x, axis=-1) * (1 + ca) + sa
    x = x + ga * _L0_attn_ref(h, L0_attn_inW_f, L0_attn_convW_f, L0_attn_convB_f, L0_attn_xpW_f, L0_attn_dtW_f, L0_attn_dtB_f, L0_attn_Alog_f, L0_attn_Dp_f, L0_attn_outW_f, L0_attn_inW_b, L0_attn_convW_b, L0_attn_convB_b, L0_attn_xpW_b, L0_attn_dtW_b, L0_attn_dtB_b, L0_attn_Alog_b, L0_attn_Dp_b, L0_attn_outW_b)
    h = _layernorm(x, axis=-1) * (1 + cb) + sb
    x = x + gb * _L0_ffn_ref(h, L0_ffn_router_w, L0_ffn_w1, L0_ffn_w2)
    return x

_drawn_inputs = setup_inputs


def setup_inputs(seed=0):
    import zlib

    import numpy as np

    out = dict(_drawn_inputs(seed))
    spreads = {'L0_attn_convB_f': (0.0, 0.8),
     'L0_attn_Dp_f': (1.0, 0.6),
     'L0_attn_convB_b': (0.0, 0.8),
     'L0_attn_Dp_b': (1.0, 0.6)}
    factors = {'L0_attn_inW_f': 8.0,
     'L0_attn_convW_f': 8.0,
     'L0_attn_xpW_f': 200.0,
     'L0_attn_dtW_f': 64.0,
     'L0_attn_dtB_f': 200.0,
     'L0_attn_Alog_f': 8.0,
     'L0_attn_outW_f': 8.0,
     'L0_attn_inW_b': 8.0,
     'L0_attn_convW_b': 8.0,
     'L0_attn_xpW_b': 64.0,
     'L0_attn_dtW_b': 64.0,
     'L0_attn_dtB_b': 200.0,
     'L0_attn_Alog_b': 8.0,
     'L0_attn_outW_b': 8.0}
    for name, (base, spread) in spreads.items():
        noise = np.random.default_rng([zlib.crc32(name.encode()), seed]).standard_normal(out[name].shape)
        drawn = base * np.exp(spread * noise) if base else spread * noise
        out[name] = jnp.asarray(drawn.astype(out[name].dtype))
    for name, factor in factors.items():
        out[name] = (out[name] * factor).astype(out[name].dtype)
    return out
```

```python
import concourse.bass as bass
from concourse import mybir
from contextlib import ExitStack

F32 = mybir.dt.float32
BF16 = mybir.dt.bfloat16
U32 = mybir.dt.uint32
ALU = mybir.AluOpType
ACT = mybir.ActivationFunctionType

P = 128
BATCH, SEQ, DM = 16, 256, 128
DI, NS, DTR, TAPS = 256, 16, 8, 4
ND = DI // P
NE, FH = 8, 256
KF = FH // P
CB = 2
CT = CB * SEQ
NCH = BATCH // CB
TT = CT // P
W = ND * CT
PAD = SEQ + 1
WP = ND * CB * PAD
NSTEP = 2 * NS
RING = 4
EPS = 1e-5
NORM = 2 * TT + 6

FIELDS = [("ct", BATCH), ("wmod", 6 * DM), ("ident", P), ("sel32", 32), ("iota8", NE),
          ("inw", 2 * 2 * DI), ("xpw", 2 * ND * P), ("dtw", 2 * DI), ("convw", 2 * ND * TAPS), ("convb", 2 * ND),
          ("dtb", 2 * ND), ("alog", 2 * ND * NS), ("dp", 2 * ND), ("rw", NE),
          ("outw", 2 * ND * DM), ("w1", NE * FH), ("w2", NE * KF * DM)]
AT, NW = {}, 0
for _name, _n in FIELDS:
    AT[_name] = (NW, NW + _n)
    NW += _n
EARLY = AT["rw"][1]

STAGE_USES = ["xiB0", "xiB1", "zB0", "out", "attT", "zB1", "ln2T", "xdB", "router", "dtB0", "dtB1",
              "ffn0", "ffn1", "ffn2", "ffn3", "ln1T", "xiF0", "xiF1", "zF0", "zF1",
              "ffn4", "ffn5", "xdF", "dtF0", "dtF1", "ffn6", "ffn7"]
AFTER = [u for u in STAGE_USES if u in ("out", "attT", "ln2T", "router") or u.startswith("ffn")]
BEFORE_B = ["xiB0", "xiB1", "zB0", "zB1", "xdB", "dtB0", "dtB1"]
BEFORE_F = ["ln1T", "xiF0", "xiF1", "zF0", "zF1", "xdF", "dtF0", "dtF1"]


def build(nc, x_l, wpack, out_l):
    ctx = ExitStack()
    with ctx:
        def sb(name, shape, dt=F32):
            return ctx.enter_context(nc.sbuf_tensor(name, shape, dt))

        def pb(name, shape=(P, CT), dt=F32):
            return ctx.enter_context(nc.psum_tensor(name, list(shape), dt))

        def sem(name):
            return ctx.enter_context(nc.semaphore(name))

        wt = sb("wt", [P, NW])

        def field(name):
            return wt[:, AT[name][0]:AT[name][1]]

        ident = field("ident")
        iota8 = field("iota8")
        inw = field("inw").rearrange("p (r e) -> p r e", r=2)
        xpw = field("xpw").rearrange("p (r k m) -> p r k m", r=2, k=ND)
        dtw = field("dtw").rearrange("p (r e) -> p r e", r=2)
        convw = field("convw").rearrange("p (r k t) -> p r k t", r=2, k=ND)
        convb = field("convb").rearrange("p (r k) -> p r k", r=2)
        dtb = field("dtb").rearrange("p (r k) -> p r k", r=2)
        dp = field("dp").rearrange("p (r k) -> p r k", r=2)
        outw = field("outw").rearrange("p (r k o) -> p r k o", r=2, k=ND)
        rw = field("rw")
        w1 = field("w1").rearrange("p (e f) -> p e f", e=NE)
        w2 = field("w2").rearrange("p (e k d) -> p e k d", e=NE, k=KF)
        selector = sb("selector", [P, 2 * NS, P], BF16)
        amat = sb("amat", [P, 2, ND, NS])
        silu_c = sb("silu_c", [P, BATCH])
        mods = sb("mods", [P, 6, BATCH])
        mod_t = sb("mod_t", [P, 2, BATCH])
        gb_rows = sb("gb_rows", [P, BATCH, DM])
        one_ln = sb("one_ln", [P, 1])
        held = sb("held", [P, 4])

        x_in = sb("x_in", [P, TT, DM])
        stats = sb("stats", [P, TT, 6])
        mv = sb("mv", [P, TT, 2])
        var = sb("var", [P, TT])
        newton = sb("newton", [P, TT])
        rstd = sb("rstd", [P, TT])
        shift = sb("shift", [P, TT])
        xn = sb("xn", [P, TT, DM])
        hT = sb("hT", [P, CT])
        xpad = sb("xpad", [P, 2, ND, CB, SEQ + TAPS - 1])
        xc = sb("xc", [P, ND, CT])
        u = sb("u", [P, 2, ND, CT])
        sz = sb("sz", [P, 2, ND, CT])
        parts = sb("parts", [P, 2, CT], BF16)
        rest = sb("rest", [P, CT])
        dt_in = sb("dt_in", [P, CT])
        sp_e = sb("sp_e", [P, ND, CT])
        sp_l = sb("sp_l", [P, ND, CT])
        sp_r = sb("sp_r", [P, ND, CT])
        delta = sb("delta", [P, 2, ND, CT])
        du = sb("du", [P, 2, ND, CT])
        b_sb = sb("b_sb", [P, RING, CT])
        decay = sb("decay", [P, RING, WP])
        drive = sb("drive", [P, RING, WP])
        state = sb("state", [P, 2, WP])
        hc = sb("hc", [P, 2, ND, CT])
        y2 = sb("y2", [P, 2, ND, CT])
        x_res = sb("x_res", [P, TT, DM])
        att = sb("att", [P, CT])
        x1 = sb("x1", [P, TT, DM])
        stats2 = sb("stats2", [P, TT, 6])
        mv2 = sb("mv2", [P, TT, 2])
        var2 = sb("var2", [P, TT])
        newton2 = sb("newton2", [P, TT])
        rstd2 = sb("rstd2", [P, TT])
        shift2 = sb("shift2", [P, TT])
        xn2 = sb("xn2", [P, TT, DM])
        h2T = sb("h2T", [P, CT])
        logits = sb("logits", [P, TT, NE])
        top = sb("top", [P, TT, 8])
        top_i = sb("top_i", [P, TT, 8], U32)
        top_f = sb("top_f", [P, TT, 2])
        gap = sb("gap", [P, TT, 1])
        gap_e = sb("gap_e", [P, TT, 1])
        gate = sb("gate", [P, TT, 3])
        pick = sb("pick", [P, 2, TT, NE])
        wexp = sb("wexp", [P, TT, NE])
        g = sb("g", [P, 2, KF, CT])
        acc = sb("acc", [P, TT, DM])
        out_t = sb("out_t", [P, TT, DM])

        ps_b = pb("ps_b")
        ps_c = [pb("ps_c0"), pb("ps_c1")]
        ps_y = [pb("ps_y0"), pb("ps_y1")]
        stage = pb("stage")
        ps_h = pb("ps_h")
        ps_o = pb("ps_o")

        def seqs(buf, r):
            return buf[:, r, :].rearrange("p (k b t) -> p k b t", k=ND, b=CB)[:, :, :, 0:SEQ]

        w_early, w_late = sem("w_early"), sem("w_late")
        x_in_loaded, x_res_loaded, stored = sem("x_in_loaded"), sem("x_res_loaded"), sem("stored")
        silu_c_done, mod_full, mods_s = sem("silu_c_done"), sem("mod_full"), sem("mods_s")
        gb_full, gb_s, gb_fix = sem("gb_full"), sem("gb_s"), sem("gb_fix")
        zeroed, pool_zeroed, a_exp, a_neg, sel_done = (sem("zeroed"), sem("pool_zeroed"), sem("a_exp"), sem("a_neg"),
                                                       sem("sel_done"))
        tick = sem("tick")
        ln1_s, xn_done, ln1_full, hT_done = sem("ln1_s"), sem("xn_done"), sem("ln1_full"), sem("hT_done")
        xi_full, xpad_done, tap0_done, conv_s = sem("xi_full"), sem("xpad_done"), sem("tap0_done"), sem("conv_s")
        z_full, z_copied, silu_s = sem("z_full"), sem("z_copied"), sem("silu_s")
        xd_full, cast_s, rest_done, split_s = sem("xd_full"), sem("cast_s"), sem("rest_done"), sem("split_s")
        dt_full, dt_act, expln_s, corr_done, delta_s = (sem("dt_full"), sem("dt_act"), sem("expln_s"),
                                                        sem("corr_done"), sem("delta_s"))
        b_full, b_copied, c_full = sem("b_full"), sem("b_copied"), sem("c_full")
        decay_done, drive_done, scan_done, hc_done, summed = (sem("decay_done"), sem("drive_done"), sem("scan_done"),
                                                              sem("hc_done"), sem("summed"))
        y_read, y2_done = sem("y_read"), sem("y2_done")
        out_full, att_done, attT_full, x1_done = sem("out_full"), sem("att_done"), sem("attT_full"), sem("x1_done")
        ln2_s, xn2_done, ln2_full, h2T_done = sem("ln2_s"), sem("xn2_done"), sem("ln2_full"), sem("h2T_done")
        router_full, logits_done, route_s, gap_done, gap_exp = (sem("router_full"), sem("logits_done"), sem("route_s"),
                                                                sem("gap_done"), sem("gap_exp"))
        h_full, gelu_done, o_full, comb_s, out_s = (sem("h_full"), sem("gelu_done"), sem("o_full"), sem("comb_s"),
                                                    sem("out_s"))
        wexp_done = sem("wexp_done")
        mid_done = sem("mid_done")
        seed1, seed2 = sem("seed1"), sem("seed2")

        def stage_reader(use, i):
            c = i - 1
            if use == "out":
                return att_done, CB * (c + 1)
            if use == "attT":
                return x1_done, c + 1
            if use == "ln2T":
                return h2T_done, CB * (c + 1)
            if use == "router":
                return logits_done, c + 1
            if use.startswith("ffn"):
                return gelu_done, 2 * NE * c + 2 * int(use[3:]) + 2
            if use == "ln1T":
                return hT_done, CB * (i + 2)
            q = 2 * i + 1 if use[2] == "B" or use[1] == "B" else 2 * i + 2
            k = int(use[-1]) if use[-1].isdigit() else 0
            if use.startswith("xi"):
                return xpad_done, ND * q + k + 1
            if use.startswith("z"):
                return z_copied, ND * q + k + 1
            if use.startswith("xd"):
                return rest_done, q + 1
            return dt_act, 2 * ND * q + 2 * (k + 1)

        def wait_stage(pe, use, i, uses, before):
            k = uses.index(use)
            s, v = stage_reader(uses[k - 1], i) if k else before
            pe.wait_ge(s, v)

        block = ctx.enter_context(nc.Block())

        @block.sync
        def _(sp):
            def load_x_in(c):
                sp.dma_start(x_in[:].rearrange("p s d -> p (s d)"), x_l[c]).then_inc(x_in_loaded, 16)

            def load_x_res(c):
                sp.dma_start(x_res[:].rearrange("p s d -> p (s d)"), x_l[c]).then_inc(x_res_loaded, 16)

            def store(c):
                sp.wait_ge(out_s, 2 * (c + 1))
                sp.dma_start(out_l[c], out_t[:].rearrange("p s d -> p (s d)")).then_inc(stored, 16)

            load_x_in(0)
            sp.dma_start(wt[:, 0:EARLY], wpack[:, 0:EARLY]).then_inc(w_early, 16)
            sp.dma_start(wt[:, EARLY:NW], wpack[:, EARLY:NW]).then_inc(w_late, 16)
            sp.wait_ge(xn_done, TT)
            load_x_in(1)
            load_x_res(0)
            with sp.Fori(1, NCH - 1) as i:
                sp.wait_ge(xn_done, TT * (i + 1))
                load_x_in(i + 1)
                sp.wait_ge(x1_done, i)
                load_x_res(i)
                store(i - 1)
            sp.wait_ge(x1_done, NCH - 1)
            load_x_res(NCH - 1)
            store(NCH - 2)
            store(NCH - 1)
            sp.wait_ge(stored, 16 * NCH)

        @block.tensor
        def _(pe):
            def transpose_tiles(dst, src):
                for s in range(TT):
                    last = nc.tensor.transpose(dst[:, s * P:(s + 1) * P], src[:, s * P:(s + 1) * P], ident)
                return last

            def ln1T(c):
                pe.wait_ge(xn_done, TT * (c + 1))
                transpose_tiles(stage, xn[:].rearrange("p s d -> p (s d)")).then_inc(ln1_full, 1)

            def xi(q, d, k, c):
                pe.wait_ge(hT_done, CB * (c + 1))
                nc.tensor.matmul(stage[:], inw[:, d, k * P:(k + 1) * P], hT[:], start=True, stop=True).then_inc(xi_full, 1)

            def zz(q, d, k):
                nc.tensor.matmul(stage[:], inw[:, d, DI + k * P:DI + (k + 1) * P], hT[:],
                                 start=True, stop=True).then_inc(z_full, 1)

            def xd(q, d):
                pe.wait_ge(silu_s, 2 * q + 2)
                for k in range(ND):
                    last = nc.tensor.matmul(stage[:], xpw[:, d, k, :], u[:, d, k, :], start=(k == 0), stop=(k == ND - 1))
                last.then_inc(xd_full, 1)

            def dt(q, d, k):
                pe.wait_ge(cast_s, 2 * q + 2)
                nc.tensor.matmul(stage[:], dtw[32:32 + DTR, d, k * P:(k + 1) * P], dt_in[32:32 + DTR, :],
                                 start=True, stop=True).then_inc(dt_full, 1)

            def bcast_b(t, q, d, n, first=False):
                if n == 0:
                    pe.wait_ge(split_s, q + 1)
                if not first:
                    pe.wait_ge(b_copied, t)
                nc.tensor.matmul(ps_b[:], selector[:, n, :], parts[:, d, :], start=True, stop=True).then_inc(b_full, 1)

            def bcast_c(t, q, d, n, first=False):
                if not first:
                    pe.wait_ge(hc_done, t - 1)
                nc.tensor.matmul(ps_c[n % 2][:], selector[:, NS + n, :], parts[:, d, :],
                                 start=True, stop=True).then_inc(c_full, 1)

            def nsum(t, q, n, first=False):
                pe.wait_ge(hc_done, t + 1)
                if n == 0 and not first:
                    pe.wait_ge(y_read, ND * q)
                for k in range(ND):
                    last = nc.tensor.matmul(ps_y[k][:], ident, hc[:, n % 2, k, :], start=(n == 0), stop=(n == NS - 1))
                last.then_inc(summed, 1)

            def outproj(c):
                pe.wait_ge(y2_done, 2 * (c + 1))
                for j in range(2 * ND):
                    d, k = j // ND, j % ND
                    last = nc.tensor.matmul(stage[:], outw[:, d, k, :], y2[:, d, k, :], start=(j == 0), stop=(j == 2 * ND - 1))
                last.then_inc(out_full, 1)

            def attT(c):
                pe.wait_ge(att_done, CB * (c + 1))
                transpose_tiles(stage, att).then_inc(attT_full, 1)

            def ln2T(c):
                pe.wait_ge(xn2_done, TT * (c + 1))
                transpose_tiles(stage, xn2[:].rearrange("p s d -> p (s d)")).then_inc(ln2_full, 1)

            def router(c):
                pe.wait_ge(h2T_done, CB * (c + 1))
                for s in range(TT):
                    last = nc.tensor.matmul(stage[:, s * NE:(s + 1) * NE], h2T[:, s * P:(s + 1) * P], rw,
                                            start=True, stop=True)
                last.then_inc(router_full, 1)

            def hidden0(c, e, first=False):
                if not first:
                    pe.wait_ge(gelu_done, 2 * NE * c + 2 * e - 1)
                nc.tensor.matmul(ps_h[:], w1[:, e, 0:P], h2T[:], start=True, stop=True).then_inc(h_full, 1)

            def hidden1(c, e):
                nc.tensor.matmul(stage[:], w1[:, e, P:2 * P], h2T[:], start=True, stop=True).then_inc(h_full, 1)

            def expert_out(c, e, first=False):
                pe.wait_ge(gelu_done, 2 * NE * c + 2 * e + 2)
                if not first:
                    pe.wait_ge(comb_s, NE * TT * c + TT * e)
                for s in range(TT):
                    for k in range(KF):
                        last = nc.tensor.matmul(ps_o[:, s * DM:(s + 1) * DM], g[:, e % 2, k, s * P:(s + 1) * P],
                                                w2[:, e, k, :], start=(k == 0), stop=(k == KF - 1))
                last.then_inc(o_full, 1)

            def side(use, i, uses, before):
                wait_stage(pe, use, i, uses, before)
                c = i - 1
                if use == "out":
                    outproj(c)
                elif use == "attT":
                    attT(c)
                elif use == "ln2T":
                    ln2T(c)
                elif use == "router":
                    router(c)
                elif use.startswith("ffn"):
                    hidden1(c, int(use[3:]))
                elif use == "ln1T":
                    ln1T(i + 1)
                else:
                    back = "B" in use
                    d, q, cc = (1, 2 * i + 1, i) if back else (0, 2 * i + 2, i + 1)
                    k = int(use[-1]) if use[-1].isdigit() else 0
                    if use.startswith("xi"):
                        xi(q, d, k, cc)
                    elif use.startswith("z"):
                        zz(q, d, k)
                    elif use.startswith("xd"):
                        xd(q, d)
                    else:
                        dt(q, d, k)

            PE_SIDE = {0: ["xiB0"], 1: ["xiB1"], 2: ["zB0"], 3: ["out"], 4: ["attT", "zB1"], 7: ["ln2T"], 8: ["xdB", "router"],
                       9: ["dtB0"], 10: ["dtB1"],
                       11: ["ffn0"], 12: ["ffn1"], 13: ["eo0"], 14: ["eo1"],
                       16: ["ffn2"], 17: ["ffn3"], 18: ["ln1T", "eo2"], 19: ["xiF0", "eo3"], 20: ["xiF1"],
                       21: ["zF0"], 22: ["zF1", "ffn4"], 23: ["ffn5"], 24: ["xdF", "eo4"], 25: ["dtF0", "eo5"],
                       26: ["dtF1"], 27: ["ffn6"], 28: ["ffn7"], 29: ["eo6"], 30: ["eo7"]}

            def iteration(i, uses, before, first=False, last=False):
                q0 = 2 * i
                if first:
                    bcast_b(0, 0, 0, 0, first=True)
                    bcast_c(0, 0, 0, 0, first=True)
                for s in range(NSTEP):
                    d, n = s // NS, s % NS
                    t = NSTEP * i + s
                    more = not (last and s == NSTEP - 1)
                    d1, n1 = ((s + 1) // NS) % 2, (s + 1) % NS
                    if more:
                        q1 = q0 + (s + 1) // NS
                        bcast_b(t + 1, q1, d1, n1)
                    for use in PE_SIDE.get(s, []):
                        if use.startswith("eo"):
                            if "ffn0" in uses:
                                e = int(use[2:])
                                expert_out(i - 1, e, first=(e == 0 and isinstance(i, int) and i == 1))
                        elif use in uses:
                            if use.startswith("ffn"):
                                e = int(use[3:])
                                hidden0(i - 1, e, first=(e == 0 and isinstance(i, int) and i == 1))
                            side(use, i, uses, before)
                    if more:
                        bcast_c(t + 1, q1, d1, n1, first=(first and s == 0))
                    if s > 0:
                        nsum(t - 1, q0 + (s - 1) // NS, (s - 1) % NS, first=(first and s == 1))
                    elif not first:
                        nsum(t - 1, q0 - 1, NS - 1)

            pe.wait_ge(silu_c_done, 1)
            for j in range(6):
                last = nc.tensor.matmul(stage[:, j * BATCH:(j + 1) * BATCH],
                                        field("wmod")[:, j * DM:(j + 1) * DM], silu_c[:], start=True, stop=True)
            last.then_inc(mod_full, 1)
            for r in range(BATCH // 4):
                if r:
                    pe.wait_ge(gb_s, r)
                for j in range(4):
                    b = 4 * r + j
                    last = nc.tensor.matmul(ps_h[:, j * DM:(j + 1) * DM], silu_c[:, b:b + 1].to_broadcast([P, P]),
                                            field("wmod")[:, 5 * DM:6 * DM], start=True, stop=True)
                last.then_inc(gb_full, 1)
            pe.wait_ge(gb_s, BATCH // 4)
            pe.wait_ge(mods_s, 1)
            for use in BEFORE_F:
                side(use, -1, BEFORE_F, (mods_s, 1))
            pe.wait_ge(sel_done, 1)
            pe.wait_ge(w_late, 16)
            iteration(0, [x for x in STAGE_USES if x not in AFTER], stage_reader("dtF1", -1), first=True)
            iteration(1, STAGE_USES, stage_reader("dtF1", 0))
            with pe.Fori(2, NCH - 1) as i:
                iteration(i, STAGE_USES, stage_reader("ffn7", i - 1))
            iteration(NCH - 1, [x for x in STAGE_USES if x not in BEFORE_F], stage_reader("ffn7", NCH - 2), last=True)
            nsum(NSTEP * NCH - 1, 2 * NCH - 1, NS - 1)
            for use in AFTER:
                if use.startswith("ffn"):
                    e = int(use[3:])
                    hidden0(NCH - 1, e)
                side(use, NCH, AFTER, stage_reader("ffn7", NCH - 1))
                if use.startswith("ffn"):
                    expert_out(NCH - 1, int(use[3:]))

        @block.scalar
        def _(act):
            def root_seed(v, rs, s_, seed_done, c):
                act.wait_ge(s_, NORM * c + 2 * TT + 1)
                nc.scalar.activation(rs[:], v[:], ACT.Ln).then_inc(seed_done, 1)
                act.wait_ge(seed_done, 2 * c + 1)
                nc.scalar.activation(rs[:], rs[:], ACT.Exp, scale=-0.5).then_inc(seed_done, 1)

            def xn1(c):
                act.wait_ge(ln1_s, NORM * (c + 1))
                for s in range(TT):
                    nc.scalar.activation(xn[:, s, :], x_in[:, s, :], ACT.Identity, scale=rstd[:, s:s + 1],
                                         bias=shift[:, s:s + 1]).then_inc(xn_done, 1)

            def modulate1(c):
                act.wait_ge(ln1_full, c + 1)
                for b in range(CB):
                    nc.scalar.activation(hT[:, b * SEQ:(b + 1) * SEQ], stage[:, b * SEQ:(b + 1) * SEQ], ACT.Identity,
                                         scale=mods[:, 1, bass.ds(CB * c + b, 1)],
                                         bias=mods[:, 0, bass.ds(CB * c + b, 1)]).then_inc(hT_done, 1)

            def xpad_copy(q, d, k):
                act.wait_ge(xi_full, ND * q + k + 1)
                at = (TAPS - 1) if d == 0 else 0
                nc.scalar.copy(xpad[:, d, k, :, at:at + SEQ],
                               stage[:].rearrange("p (b t) -> p b t", b=CB)).then_inc(xpad_done, 1)

            def tap0(q, d, k, first=False):
                act.wait_ge(xpad_done, ND * q + k + 1)
                if k == 0 and not first:
                    act.wait_ge(delta_s, 4 * (q - 1) + 1)
                at = 0 if d == 0 else TAPS - 1
                nc.scalar.activation(xc[:, k, :].rearrange("p (b t) -> p b t", b=CB), xpad[:, d, k, :, at:at + SEQ],
                                     ACT.Identity, scale=convw[:, d, k, 0:1], bias=convb[:, d, k:k + 1]
                                     ).then_inc(tap0_done, 1)

            def z_copy(q, d, k, first=False):
                act.wait_ge(z_full, ND * q + k + 1)
                if not first:
                    act.wait_ge(y2_done, q - 1)
                nc.scalar.copy(sz[:, d, k, :], stage[:]).then_inc(z_copied, 1)

            def silus(q, d):
                act.wait_ge(z_copied, ND * (q + 1))
                nc.scalar.activation(sz[:, d], sz[:, d], ACT.Silu).then_inc(silu_s, 1)
                act.wait_ge(conv_s, ND * (TAPS - 1) * (q + 1))
                nc.scalar.activation(u[:, d], xc[:], ACT.Silu).then_inc(silu_s, 1)

            def to_exp_ln():
                nc.scalar.activation(one_ln[0:1, 0:1], ident[0:1, 0:1], ACT.Ln).then_inc(tick, 1)

            def casts(q, d):
                act.wait_ge(xd_full, q + 1)
                nc.scalar.copy(dt_in[32:32 + DTR, :], stage[32:32 + DTR, :]).then_inc(cast_s, 1)
                nc.scalar.copy(parts[:, d, :], stage[:]).then_inc(cast_s, 1)

            def dt_acts(q, d, k, first=False):
                act.wait_ge(dt_full, ND * q + k + 1)
                if k == 0 and not first:
                    act.wait_ge(delta_s, 4 * (q - 1) + 3)
                nc.scalar.activation(sp_e[:, k, :], stage[:], ACT.Abs, bias=dtb[:, d, k:k + 1]).then_inc(dt_act, 1)
                nc.scalar.activation(sp_r[:, k, :], stage[:], ACT.Relu, bias=dtb[:, d, k:k + 1]).then_inc(dt_act, 1)

            def exp_ln(q):
                act.wait_ge(dt_act, 2 * ND * (q + 1))
                nc.scalar.activation(sp_e[:], sp_e[:], ACT.Exp, scale=-1.0).then_inc(expln_s, 1)
                act.wait_ge(expln_s, 2 * q + 1)
                nc.scalar.activation(sp_l[:], sp_e[:], ACT.Ln, bias=1.0).then_inc(expln_s, 1)

            def step(t, q, d, n, head):
                r = n % RING
                act.wait_ge(b_full, t + 1)
                if head >= RING:
                    act.wait_ge(drive_done, t - RING + 1)
                nc.scalar.copy(b_sb[:, r, :], ps_b[:]).then_inc(b_copied, 1)
                if n == 0:
                    act.wait_ge(delta_s, 4 * q + 3)
                if head >= RING:
                    act.wait_ge(scan_done, t - RING + 1)
                else:
                    act.wait_ge(zeroed, 1)
                for k in range(ND):
                    nc.scalar.activation(seqs(decay, r)[:, k], delta[:, d, k, :].rearrange("p (b t) -> p b t", b=CB),
                                         ACT.Exp, scale=amat[:, d, k, n:n + 1]).then_inc(decay_done, 1)

            def att_scale(c):
                act.wait_ge(out_full, c + 1)
                for b in range(CB):
                    nc.scalar.activation(att[:, b * SEQ:(b + 1) * SEQ], stage[:, b * SEQ:(b + 1) * SEQ], ACT.Identity,
                                         scale=mods[:, 2, bass.ds(CB * c + b, 1)]).then_inc(att_done, 1)

            def xn2_(c):
                act.wait_ge(ln2_s, NORM * (c + 1))
                for s in range(TT):
                    nc.scalar.activation(xn2[:, s, :], x1[:, s, :], ACT.Identity, scale=rstd2[:, s:s + 1],
                                         bias=shift2[:, s:s + 1]).then_inc(xn2_done, 1)

            def modulate2(c):
                act.wait_ge(ln2_full, c + 1)
                for b in range(CB):
                    nc.scalar.activation(h2T[:, b * SEQ:(b + 1) * SEQ], stage[:, b * SEQ:(b + 1) * SEQ], ACT.Identity,
                                         scale=mods[:, 4, bass.ds(CB * c + b, 1)],
                                         bias=mods[:, 3, bass.ds(CB * c + b, 1)]).then_inc(h2T_done, 1)

            def gate_exp(c):
                act.wait_ge(gap_done, c + 1)
                nc.scalar.activation(gap_e[:], gap[:], ACT.Exp).then_inc(gap_exp, 1)

            def gelus(c, e, e_first):
                for k in range(KF):
                    act.wait_ge(h_full, 2 * NE * c + 2 * e + k + 1)
                    if k == 0 and not e_first:
                        act.wait_ge(o_full, NE * c + e - 1)
                    nc.scalar.activation(g[:, e % 2, k, :], (ps_h if k == 0 else stage)[:], ACT.Gelu).then_inc(gelu_done, 1)

            def side(s, i, after=True, before=True, first=False, second=False):
                c = i - 1
                qb, qf = 2 * i + 1, 2 * i + 2
                if s == 0:
                    xpad_copy(qb, 1, 0)
                elif s == 1:
                    xpad_copy(qb, 1, 1)
                    tap0(qb, 1, 0)
                elif s == 2:
                    tap0(qb, 1, 1)
                    z_copy(qb, 1, 0, first)
                elif s == 3 and after:
                    att_scale(c)
                elif s == 4:
                    z_copy(qb, 1, 1, first)
                elif s == 5 and after:
                    root_seed(var2, rstd2, ln2_s, seed2, c)
                elif s == 6 and after:
                    xn2_(c)
                elif s == 7:
                    if after:
                        modulate2(c)
                    silus(qb, 1)
                    to_exp_ln()
                elif s == 8:
                    casts(qb, 1)
                elif s == 9:
                    dt_acts(qb, 1, 0)
                    if after:
                        gate_exp(c)
                elif s == 10:
                    dt_acts(qb, 1, 1)
                    exp_ln(qb)
                elif s in (12, 17, 23, 28):
                    e0 = {12: 0, 17: 2, 23: 4, 28: 6}[s]
                    if s == 17 and before:
                        xn1(i + 1)
                    if s == 23 and before:
                        silus(qf, 0)
                    if after:
                        gelus(c, e0, second and e0 < 2)
                        gelus(c, e0 + 1, second and e0 < 2)
                    if after or (s == 23 and before):
                        to_exp_ln()
                elif not before:
                    return
                elif s == 16:
                    root_seed(var, rstd, ln1_s, seed1, i + 1)
                elif s == 18:
                    modulate1(i + 1)
                elif s == 19:
                    xpad_copy(qf, 0, 0)
                elif s == 20:
                    xpad_copy(qf, 0, 1)
                    tap0(qf, 0, 0)
                elif s == 21:
                    tap0(qf, 0, 1)
                    z_copy(qf, 0, 0)
                elif s == 22:
                    z_copy(qf, 0, 1)
                elif s == 24:
                    casts(qf, 0)
                elif s == 25:
                    dt_acts(qf, 0, 0)
                elif s == 26:
                    dt_acts(qf, 0, 1)
                    exp_ln(qf)

            def iteration(i, first=False, **kw):
                for s in range(NSTEP):
                    step(NSTEP * i + s, 2 * i + s // NS, s // NS, s % NS, s if first else RING)
                    side(s, i, first=first, **kw)

            act.wait_ge(w_early, 16)
            nc.scalar.activation(silu_c[:], field("ct"), ACT.Silu).then_inc(silu_c_done, 1)
            act.wait_ge(mod_full, 1)
            nc.scalar.copy(mods[:].rearrange("p j b -> p (j b)"), stage[:, 0:6 * BATCH]).then_inc(mods_s, 1)
            for r in range(BATCH // 4):
                act.wait_ge(gb_full, r + 1)
                nc.scalar.copy(gb_rows[:, 4 * r:4 * r + 4, :].rearrange("p b d -> p (b d)"), ps_h[:]).then_inc(gb_s, 1)
            root_seed(var, rstd, ln1_s, seed1, 0)
            xn1(0)
            act.wait_ge(mods_s, 6)
            modulate1(0)
            act.wait_ge(pool_zeroed, 1)
            xpad_copy(0, 0, 0)
            xpad_copy(0, 0, 1)
            tap0(0, 0, 0, True)
            tap0(0, 0, 1)
            z_copy(0, 0, 0, True)
            z_copy(0, 0, 1, True)
            silus(0, 0)
            to_exp_ln()
            nc.scalar.activation(amat[:].rearrange("p r k n -> p (r k n)"), field("alog"), ACT.Exp).then_inc(a_exp, 1)
            casts(0, 0)
            dt_acts(0, 0, 0, True)
            dt_acts(0, 0, 1)
            exp_ln(0)
            act.wait_ge(a_neg, 1)
            iteration(0, first=True, after=False)
            iteration(1, second=True)
            with act.Fori(2, NCH - 1) as i:
                iteration(i)
            iteration(NCH - 1, before=False)
            c = NCH - 1
            att_scale(c)
            root_seed(var2, rstd2, ln2_s, seed2, c)
            xn2_(c)
            modulate2(c)
            gate_exp(c)
            for e in range(NE):
                gelus(c, e, False)

        @block.vector
        def _(dve):
            def norm_stats(src, st, m, v, s_, hold, c):
                for s in range(TT):
                    nc.vector.bn_stats(st[:, s, :], src[:, s, :]).then_inc(s_, 1)
                dve.wait_ge(s_, NORM * c + TT)
                nc.vector.memset(held[0:1, hold:hold + 1], 0.0)
                for s in range(TT):
                    nc.vector.bn_aggr(m[:, s, :], st[:, s, :]).then_inc(s_, 1)
                dve.wait_ge(s_, NORM * c + 2 * TT)
                nc.vector.tensor_scalar(v[:], m[:, :, 1], EPS, None, ALU.add).then_inc(s_, 1)

            def norm_root(m, v, rs, tmp, sh, s_, seed_done, c):
                n0 = NORM * c + 2 * TT + 1
                dve.wait_ge(seed_done, 2 * (c + 1))
                nc.vector.tensor_tensor(tmp[:], rs[:], rs[:], ALU.mult).then_inc(s_, 1)
                dve.wait_ge(s_, n0 + 1)
                nc.vector.tensor_tensor(tmp[:], tmp[:], v[:], ALU.mult).then_inc(s_, 1)
                dve.wait_ge(s_, n0 + 2)
                nc.vector.tensor_scalar(tmp[:], tmp[:], -0.5, 1.5, ALU.mult, ALU.add).then_inc(s_, 1)
                dve.wait_ge(s_, n0 + 3)
                nc.vector.tensor_tensor(rs[:], rs[:], tmp[:], ALU.mult).then_inc(s_, 1)
                dve.wait_ge(s_, n0 + 4)
                nc.vector.scalar_tensor_tensor(out=sh[:], in0=m[:, :, 0], scalar=-1.0, in1=rs[:], op0=ALU.mult,
                                               op1=ALU.mult).then_inc(s_, 1)

            def ln1(c, first=False):
                dve.wait_ge(x_in_loaded, 16 * (c + 1))
                if not first:
                    dve.wait_ge(xn_done, TT * c)
                norm_stats(x_in, stats, mv, var, ln1_s, 0, c)

            def ln1_root(c):
                norm_root(mv, var, rstd, newton, shift, ln1_s, seed1, c)

            def taps(q, d, k):
                v = xc[:, k, :].rearrange("p (b t) -> p b t", b=CB)
                for j in range(1, TAPS):
                    if j == 1:
                        dve.wait_ge(tap0_done, ND * q + k + 1)
                    else:
                        dve.wait_ge(conv_s, (TAPS - 1) * (ND * q + k) + j - 1)
                    at = j if d == 0 else TAPS - 1 - j
                    nc.vector.scalar_tensor_tensor(out=v, in0=xpad[:, d, k, :, at:at + SEQ],
                                                   scalar=convw[:, d, k, j:j + 1], in1=v, op0=ALU.mult,
                                                   op1=ALU.add).then_inc(conv_s, 1)

            def residue(q, d):
                dve.wait_ge(cast_s, 2 * (q + 1))
                nc.vector.tensor_tensor(rest[64:128, :], stage[64:128, :], parts[64:128, d, :],
                                        ALU.subtract).then_inc(rest_done, 1)
                dve.wait_ge(rest_done, q + 1)
                nc.vector.tensor_copy(parts[64:128, d, :], rest[64:128, :]).then_inc(mid_done, 1)
                dve.wait_ge(mid_done, q + 1)
                nc.vector.tensor_tensor(parts[96:128, d, :], rest[96:128, :], parts[96:128, d, :],
                                        ALU.subtract).then_inc(split_s, 1)

            def correction(q):
                dve.wait_ge(expln_s, 2 * q + 1)
                nc.vector.tensor_scalar(xc[:], sp_e[:], 1.0, -1.0, ALU.add, ALU.add).then_inc(corr_done, 1)

            def scan(t, q, d, n, head):
                r = n % RING
                dve.wait_ge(decay_done, ND * (t + 1))
                dve.wait_ge(drive_done, t + 1)
                if head >= 2:
                    dve.wait_ge(hc_done, t - 1)
                rng = slice(None, None, -1) if d else slice(None)
                nc.vector.tensor_tensor_scan(state[:, n % 2, 0:WP - 1][:, rng], decay[:, r, 0:WP - 1][:, rng],
                                             drive[:, r, 0:WP - 1][:, rng], 0.0, ALU.mult, ALU.add).then_inc(scan_done, 1)

            def times_c(t, n, head):
                dve.wait_ge(scan_done, t + 1)
                dve.wait_ge(c_full, t + 1)
                if head >= 2:
                    dve.wait_ge(summed, t - 1)
                nc.vector.tensor_tensor(hc[:, n % 2].rearrange("p k (b t) -> p k b t", b=CB), seqs(state, n % 2),
                                        ps_c[n % 2][:].rearrange("p (b t) -> p b t", b=CB).unsqueeze(1)
                                        .to_broadcast([P, ND, CB, SEQ]), ALU.mult).then_inc(hc_done, 1)

            def residual(c):
                dve.wait_ge(attT_full, c + 1)
                dve.wait_ge(x_res_loaded, 16 * (c + 1))
                if not (isinstance(c, int) and c == 0):
                    dve.wait_ge(out_s, 2 * c)
                nc.vector.tensor_tensor(x1[:].rearrange("p s d -> p (s d)"), stage[:],
                                        x_res[:].rearrange("p s d -> p (s d)"), ALU.add).then_inc(x1_done, 1)

            def ln2(c):
                dve.wait_ge(x1_done, c + 1)
                norm_stats(x1, stats2, mv2, var2, ln2_s, 1, c)

            def ln2_root(c):
                norm_root(mv2, var2, rstd2, newton2, shift2, ln2_s, seed2, c)

            def route_a(c):
                dve.wait_ge(router_full, c + 1)
                nc.vector.tensor_copy(logits[:].rearrange("p s e -> p (s e)"), stage[:, 0:TT * NE]).then_inc(logits_done, 1)
                dve.wait_ge(logits_done, c + 1)
                nc.vector.memset(held[0:1, 2:3], 0.0)
                n0 = 2 * TT + 7
                for s in range(TT):
                    nc.vector.max(top[:, s, :], logits[:, s, :]).then_inc(route_s, 1)
                dve.wait_ge(route_s, n0 * c + TT)
                nc.vector.memset(held[0:1, 3:4], 0.0)
                for s in range(TT):
                    nc.vector.max_index(top_i[:, s, :], top[:, s, :], logits[:, s, :]).then_inc(route_s, 1)
                nc.vector.tensor_tensor(gap[:], top[:, :, 1:2], top[:, :, 0:1], ALU.subtract).then_inc(gap_done, 1)
                dve.wait_ge(route_s, n0 * c + 2 * TT)
                nc.vector.tensor_copy(top_f[:], top_i[:, :, 0:2]).then_inc(route_s, 1)

            def route_b(c):
                n0 = 2 * TT + 7
                k0 = n0 * c + 2 * TT + 1
                dve.wait_ge(gap_exp, c + 1)
                nc.vector.tensor_scalar(gate[:, :, 0:1], gap_e[:], 1.0, None, ALU.add).then_inc(route_s, 1)
                dve.wait_ge(route_s, k0 + 1)
                nc.vector.reciprocal(gate[:, :, 1:2], gate[:, :, 0:1]).then_inc(route_s, 1)
                dve.wait_ge(route_s, k0 + 2)
                nc.vector.tensor_tensor(gate[:, :, 2:3], gate[:, :, 1:2], gap_e[:], ALU.mult).then_inc(route_s, 1)
                for j in range(2):
                    nc.vector.tensor_tensor(pick[:, j], iota8.unsqueeze(1).to_broadcast([P, TT, NE]),
                                            top_f[:, :, j:j + 1].to_broadcast([P, TT, NE]), ALU.is_equal).then_inc(route_s, 1)
                dve.wait_ge(route_s, k0 + 5)
                nc.vector.tensor_tensor(pick[:].rearrange("p j s e -> p s j e"), pick[:].rearrange("p j s e -> p s j e"),
                                        gate[:, :, 1:3].unsqueeze(3).to_broadcast([P, TT, 2, NE]),
                                        ALU.mult).then_inc(route_s, 1)
                dve.wait_ge(route_s, k0 + 6)
                nc.vector.tensor_tensor(wexp[:], pick[:, 0], pick[:, 1], ALU.add).then_inc(wexp_done, 1)

            def combine(c, e):
                dve.wait_ge(o_full, NE * c + e + 1)
                if e == 0:
                    dve.wait_ge(wexp_done, c + 1)
                    if not (isinstance(c, int) and c == 0):
                        dve.wait_ge(out_s, 2 * c)
                else:
                    dve.wait_ge(comb_s, NE * TT * c + TT * e)
                for s in range(TT):
                    src = ps_o[:, s * DM:(s + 1) * DM]
                    if e == 0:
                        nc.vector.tensor_scalar(acc[:, s, :], src, wexp[:, s, 0:1], None, ALU.mult).then_inc(comb_s, 1)
                    else:
                        nc.vector.scalar_tensor_tensor(out=acc[:, s, :], in0=src, scalar=wexp[:, s, e:e + 1],
                                                       in1=acc[:, s, :], op0=ALU.mult, op1=ALU.add).then_inc(comb_s, 1)

            def side(s, i, after=True, before=True, first=False):
                c = i - 1
                qb, qf = 2 * i + 1, 2 * i + 2
                if s == 1 and after:
                    y_out_b(c)
                elif s == 2:
                    taps(qb, 1, 0)
                elif s == 3:
                    taps(qb, 1, 1)
                elif s == 4 and after:
                    residual(c)
                    ln2(c)
                elif s == 5 and after:
                    ln2_root(c)
                elif s == 8:
                    residue(qb, 1)
                    if after:
                        route_a(c)
                elif s == 10 and after:
                    route_b(c)
                elif s == 11:
                    correction(qb)
                elif s == 15 and before:
                    ln1(i + 1)
                elif s == 16 and before:
                    ln1_root(i + 1)
                elif s == 17:
                    y_out_f(i)
                elif s == 21 and before:
                    taps(qf, 0, 0)
                elif s == 22 and before:
                    taps(qf, 0, 1)
                elif s == 24 and before:
                    residue(qf, 0)
                elif s == 27 and before:
                    correction(qf)
                e = {13: 0, 14: 1, 18: 2, 19: 3, 24: 4, 25: 5, 29: 6, 30: 7}.get(s)
                if e is not None and after:
                    combine(c, e)

            def y_out_b(c):
                y_pass(2 * c + 1, 1, c)

            def y_out_f(c):
                y_pass(2 * c, 0, c)

            def y_pass(q, d, c):
                dve.wait_ge(summed, NS * (q + 1))
                if not (isinstance(c, int) and c == 0):
                    dve.wait_ge(out_full, c)
                for k in range(ND):
                    nc.vector.scalar_tensor_tensor(out=y2[:, d, k, :], in0=u[:, d, k, :], scalar=dp[:, d, k:k + 1],
                                                   in1=ps_y[k][:], op0=ALU.mult, op1=ALU.add).then_inc(y_read, 1)

            def iteration(i, first=False, **kw):
                for s in range(NSTEP):
                    t = NSTEP * i + s
                    scan(t, 2 * i + s // NS, s // NS, s % NS, s if first else RING)
                    if not (first and s == 0):
                        times_c(t - 1, (s - 1) % NS, s - 1 if first else RING)
                    side(s, i, first=first, **kw)

            ln1(0, first=True)
            ln1_root(0)
            nc.vector.memset(decay[:], 0.0)
            nc.vector.memset(drive[:], 0.0).then_inc(zeroed, 1)
            dve.wait_ge(mods_s, 1)
            nc.vector.tensor_scalar(mods[:, 1], mods[:, 1], 1.0, None, ALU.add).then_inc(mods_s, 1)
            nc.vector.tensor_scalar(mods[:, 4], mods[:, 4], 1.0, None, ALU.add).then_inc(mods_s, 1)
            nc.vector.scalar_tensor_tensor(out=mod_t[:, 0], in0=mods[:, 2], scalar=-1.0, in1=mods[:, 2], op0=ALU.mult,
                                           op1=ALU.max).then_inc(mods_s, 1)
            nc.vector.tensor_scalar(mod_t[:, 1], mods[:, 2], 0.0, 0.5, ALU.is_ge, ALU.subtract).then_inc(mods_s, 1)
            dve.wait_ge(mods_s, 5)
            nc.vector.scalar_tensor_tensor(out=mods[:, 2], in0=mod_t[:, 0], scalar=0.25, in1=mod_t[:, 1], op0=ALU.max,
                                           op1=ALU.mult).then_inc(mods_s, 1)
            dve.wait_ge(w_early, 16)
            nc.vector.tensor_copy(selector[:], field("sel32").unsqueeze(2).to_broadcast([P, 2 * NS, P])).then_inc(sel_done, 1)
            taps(0, 0, 0)
            taps(0, 0, 1)
            residue(0, 0)
            correction(0)
            dve.wait_ge(a_exp, 1)
            nc.vector.tensor_scalar(amat[:].rearrange("p r k n -> p (r k n)"),
                                    amat[:].rearrange("p r k n -> p (r k n)"), -1.0, None, ALU.mult).then_inc(a_neg, 1)
            dve.wait_ge(gb_s, BATCH // 4)
            hv = hc[:].rearrange("p a k t -> p (a k t)")
            gv = gb_rows[:].rearrange("p b d -> p (b d)")
            nc.vector.scalar_tensor_tensor(out=hv, in0=gv, scalar=-1.0, in1=gv, op0=ALU.mult, op1=ALU.max).then_inc(gb_fix, 1)
            dve.wait_ge(gb_fix, 1)
            nc.vector.tensor_scalar(gv, gv, 0.0, 0.5, ALU.is_ge, ALU.subtract).then_inc(gb_fix, 1)
            dve.wait_ge(gb_fix, 2)
            nc.vector.tensor_scalar(hv, hv, 0.25, 2.0, ALU.max, ALU.mult).then_inc(gb_fix, 1)
            dve.wait_ge(gb_fix, 3)
            nc.vector.tensor_tensor(gv, gv, hv, ALU.mult).then_inc(gb_fix, 1)
            dve.wait_ge(gb_fix, 4)
            iteration(0, first=True, after=False)
            iteration(1)
            with dve.Fori(2, NCH - 1) as i:
                iteration(i)
            iteration(NCH - 1, before=False)
            times_c(NSTEP * NCH - 1, NS - 1, RING)
            c = NCH - 1
            y_out_b(c)
            residual(c)
            ln2(c)
            ln2_root(c)
            route_a(c)
            route_b(c)
            for e in range(NE):
                combine(c, e)

        @block.gpsimd
        def _(pool):
            def deltas(q, d):
                pool.wait_ge(expln_s, 2 * (q + 1))
                pool.wait_ge(corr_done, q + 1)
                nc.gpsimd.tensor_tensor(sp_e[:], sp_e[:], xc[:], ALU.subtract).then_inc(delta_s, 1)
                pool.wait_ge(delta_s, 4 * q + 1)
                nc.gpsimd.tensor_tensor(sp_e[:], sp_e[:], sp_l[:], ALU.add).then_inc(delta_s, 1)
                pool.wait_ge(delta_s, 4 * q + 2)
                nc.gpsimd.tensor_tensor(delta[:, d], sp_e[:], sp_r[:], ALU.add).then_inc(delta_s, 1)
                pool.wait_ge(delta_s, 4 * q + 3)
                nc.gpsimd.tensor_tensor(du[:, d], delta[:, d], u[:, d], ALU.mult).then_inc(delta_s, 1)

            def drive_step(t, q, d, n, head):
                r = n % RING
                pool.wait_ge(b_copied, t + 1)
                if n == 0:
                    pool.wait_ge(delta_s, 4 * (q + 1))
                if head >= RING:
                    pool.wait_ge(scan_done, t - RING + 1)
                else:
                    pool.wait_ge(zeroed, 1)
                nc.gpsimd.tensor_tensor(seqs(drive, r), du[:, d].rearrange("p k (b t) -> p k b t", b=CB),
                                        b_sb[:, r, :].rearrange("p (b t) -> p b t", b=CB).unsqueeze(1)
                                        .to_broadcast([P, ND, CB, SEQ]), ALU.mult).then_inc(drive_done, 1)

            def gate_y(q, d):
                pool.wait_ge(y_read, ND * (q + 1))
                nc.gpsimd.tensor_tensor(y2[:, d], y2[:, d], sz[:, d], ALU.mult).then_inc(y2_done, 1)

            def finish(c):
                pool.wait_ge(comb_s, NE * TT * (c + 1))
                if not (isinstance(c, int) and c == 0):
                    pool.wait_ge(stored, 16 * c)
                nc.gpsimd.tensor_tensor(out_t[:].rearrange("p (b s) d -> p b s d", b=CB),
                                        acc[:].rearrange("p (b s) d -> p b s d", b=CB),
                                        gb_rows[:, bass.ds(CB * c, CB), :].unsqueeze(2)
                                        .to_broadcast([P, CB, TT // CB, DM]), ALU.mult).then_inc(out_s, 1)
                pool.wait_ge(out_s, 2 * c + 1)
                nc.gpsimd.tensor_tensor(out_t[:], out_t[:], x1[:], ALU.add).then_inc(out_s, 1)

            def iteration(i, first=False, after=True, before=True):
                for s in range(NSTEP):
                    drive_step(NSTEP * i + s, 2 * i + s // NS, s // NS, s % NS, s if first else RING)
                    if s == 1 and after:
                        gate_y(2 * i - 1, 1)
                    elif s == 11:
                        deltas(2 * i + 1, 1)
                    elif s == 17:
                        gate_y(2 * i, 0)
                    elif s == 27 and before:
                        deltas(2 * i + 2, 0)
                    elif s == 31 and after:
                        finish(i - 1)

            nc.gpsimd.memset(xpad[:], 0.0).then_inc(pool_zeroed, 1)
            deltas(0, 0)
            iteration(0, first=True, after=False)
            iteration(1)
            pool.wait_ge(gb_fix, 4)
            with pool.Fori(2, NCH - 1) as i:
                iteration(i)
            iteration(NCH - 1, before=False)
            gate_y(2 * NCH - 1, 1)
            finish(NCH - 1)


def kernel(**inputs):
    import numpy as np
    import concourse.bacc as bacc
    from concourse.bass_utils import run_bass_kernel_spmd as run

    a = {k: np.asarray(v) for k, v in inputs.items()}
    pack = np.zeros((P, NW), np.float32)

    def put(name, value):
        lo, hi = AT[name]
        pack[:, lo:hi] = value.reshape(P, hi - lo)

    def both(name):
        return [a[f"L0_attn_{name}_f"], a[f"L0_attn_{name}_b"]]

    def channels(v):
        return v.reshape(ND, P, -1).transpose(1, 0, 2)

    put("ct", a["L0_c"].T)
    put("wmod", a["L0_wmod"])
    put("ident", np.eye(P, dtype=np.float32))
    sel = np.zeros((P, 32), np.float32)
    for base in (0, 64, 96):
        sel[base:base + 32] = np.eye(32, dtype=np.float32)
    put("sel32", sel)
    put("iota8", np.tile(np.arange(NE, dtype=np.float32), (P, 1)))
    put("inw", np.stack([v.T for v in both("inW")], 1))
    xp = np.zeros((P, 2, ND, P), np.float32)
    for d, v in enumerate(both("xpW")):
        cols = channels(v.T)
        for base in (0, 64, 96):
            xp[:, d, :, base:base + 2 * NS] = cols[:, :, DTR:]
        xp[:, d, :, 32:32 + DTR] = cols[:, :, :DTR]
    put("xpw", xp)
    dtw = np.zeros((P, 2, DI), np.float32)
    for d, v in enumerate(both("dtW")):
        dtw[32:32 + DTR, d] = v.T
    put("dtw", dtw)
    put("convw", np.stack([channels(v.reshape(DI, TAPS)) for v in both("convW")], 1))
    put("convb", np.stack([channels(v)[:, :, 0] for v in both("convB")], 1))
    put("dtb", np.stack([channels(v)[:, :, 0] for v in both("dtB")], 1))
    put("alog", np.stack([channels(v) for v in both("Alog")], 1))
    put("dp", np.stack([channels(v)[:, :, 0] for v in both("Dp")], 1))
    put("rw", a["L0_ffn_router_w"].T)
    put("outw", np.stack([channels(v.T) for v in both("outW")], 1))
    put("w1", a["L0_ffn_w1"].transpose(1, 0, 2))
    put("w2", a["L0_ffn_w2"].reshape(NE, KF, P, DM).transpose(2, 0, 1, 3))
    x_l = np.ascontiguousarray(a["L0_attn_x"].reshape(NCH, TT, P, DM).transpose(0, 2, 1, 3)).reshape(NCH, P, TT * DM)

    nc = bacc.Bacc("TRN2", target_bir_lowering=False, num_devices=1)
    arrays = {"x_l": x_l, "wpack": pack}
    args = [nc.dram_tensor(k, v.shape, mybir.dt.from_np(v.dtype), kind="ExternalInput").ap() for k, v in arrays.items()]
    args.append(nc.dram_tensor("out_l", x_l.shape, F32, kind="ExternalOutput").ap())
    build(nc, *args)
    r = run(nc, [arrays], core_ids=[0])
    return np.asarray(r.results[0]["out_l"]).reshape(NCH, P, TT, DM).transpose(0, 2, 1, 3).reshape(BATCH, SEQ, DM)
```

```python
import concourse.bass as bass
from concourse import mybir
from contextlib import ExitStack

F32 = mybir.dt.float32
BF16 = mybir.dt.bfloat16
U32 = mybir.dt.uint32
ALU = mybir.AluOpType
ACT = mybir.ActivationFunctionType

P = 128
BATCH, SEQ, DM = 16, 256, 128
DI, NS, DTR, TAPS = 256, 16, 8, 4
ND = DI // P
NE, FH = 8, 256
KF = FH // P
CB = 2
CT = CB * SEQ
NCH = BATCH // CB
TT = CT // P
W = ND * CT
PAD = SEQ + 1
WP = ND * CB * PAD
NSTEP = 2 * NS
RING = 4
LEAD = 3
DPARTS = 3
GB = 4
EPS = 1e-5
NORM = 2 * TT + 6

FIELDS = [("ident", P), ("sel32", 32), ("iota8", NE),
          ("inw", 2 * 2 * DI), ("xpw", 2 * ND * P), ("dtw", 2 * DI), ("convw", 2 * ND * TAPS), ("convb", 2 * ND),
          ("dtb", 2 * ND), ("alog", 2 * ND * NS), ("dp", 2 * ND), ("rw", NE),
          ("outw", 2 * ND * DM), ("w1", NE * FH), ("w2", NE * KF * DM)]
AT, NW = {}, 0
for _name, _n in FIELDS:
    AT[_name] = (NW, NW + _n)
    NW += _n
EARLY = AT["rw"][1]

BANK_USES = {
    "stage": ["xiB0", "zB0", "out", "dtB0", "ln2T", "ffn0", "ffn1", "ffn2", "ffn3", "xiF0", "zF0", "ffn4", "dtF0", "ffn5",
              "ffn6", "ffn7"],
    "stage2": ["xiB1", "zB1", "attT", "dtB1", "router", "ln1T", "xiF1", "zF1", "dtF1"],
    "ps_h": ["xdB", "ffn0", "ffn1", "ffn2", "ffn3", "ffn4", "xdF", "ffn5", "ffn6", "ffn7"]}
EVERY_USE = [use for uses in BANK_USES.values() for use in uses]
AFTER = ["out", "attT", "ln2T", "router"] + [f"ffn{e}" for e in range(NE)]
BEFORE_F = ["ln1T", "xiF0", "xiF1", "zF0", "zF1", "xdF", "dtF0", "dtF1"]


def build(nc, x_l, modpack, wpack, b_rows, out_l):
    ctx = ExitStack()
    with ctx:
        def sb(name, shape, dt=F32):
            return ctx.enter_context(nc.sbuf_tensor(name, shape, dt))

        def pb(name, shape=(P, CT), dt=F32):
            return ctx.enter_context(nc.psum_tensor(name, list(shape), dt))

        def sem(name):
            return ctx.enter_context(nc.semaphore(name))

        wt = sb("wt", [P, NW])

        def field(name):
            return wt[:, AT[name][0]:AT[name][1]]

        ident = field("ident")
        iota8 = field("iota8")
        inw = field("inw").rearrange("p (r e) -> p r e", r=2)
        xpw = field("xpw").rearrange("p (r k m) -> p r k m", r=2, k=ND)
        dtw = field("dtw").rearrange("p (r e) -> p r e", r=2)
        convw = field("convw").rearrange("p (r k t) -> p r k t", r=2, k=ND)
        convb = field("convb").rearrange("p (r k) -> p r k", r=2)
        dtb = field("dtb").rearrange("p (r k) -> p r k", r=2)
        dp = field("dp").rearrange("p (r k) -> p r k", r=2)
        outw = field("outw").rearrange("p (r k o) -> p r k o", r=2, k=ND)
        rw = field("rw")
        w1 = field("w1").rearrange("p (e f) -> p e f", e=NE)
        w2 = field("w2").rearrange("p (e k d) -> p e k d", e=NE, k=KF)
        selector = sb("selector", [P, 2 * NS, P], BF16)
        amat = sb("amat", [P, 2, ND, NS])
        silu_c = sb("silu_c", [P, BATCH])
        mods = sb("mods", [P, 6, BATCH])
        mod_t = sb("mod_t", [P, 2, BATCH])
        gb_rows = sb("gb_rows", [P, BATCH, DM])
        minus_half = sb("minus_half", [P, TT])
        held = sb("held", [P, 4])

        x_in = sb("x_in", [P, TT, DM])
        stats = sb("stats", [P, TT, 6])
        mv = sb("mv", [P, TT, 2])
        var = sb("var", [P, TT])
        newton = sb("newton", [P, TT])
        rstd = sb("rstd", [P, TT])
        shift = sb("shift", [P, TT])
        xn = sb("xn", [P, TT, DM])
        hT = sb("hT", [P, CT])
        xpad = sb("xpad", [P, 2, ND, CB, SEQ + TAPS - 1])
        xc = sb("xc", [P, ND, CT])
        u = sb("u", [P, 2, ND, CT])
        sz = sb("sz", [P, 2, ND, CT])
        parts = sb("parts", [P, 2, CT], BF16)
        rest = sb("rest", [P, CT])
        xdbl = sb("xdbl", [P, CT])
        sp_e = sb("sp_e", [P, ND, CT])
        sp_l = sb("sp_l", [P, ND, CT])
        sp_r = sb("sp_r", [P, ND, CT])
        delta = sb("delta", [P, 2, ND, CT])
        du = sb("du", [P, 2, ND, CT])
        b_sb = sb("b_sb", [P, RING, CT])
        decay = sb("decay", [P, RING, WP])
        drive = sb("drive", [P, RING, WP])
        state = sb("state", [P, 2, WP])
        hc = sb("hc", [P, 2, ND, CT])
        ct = state[:, 0, 0:BATCH]
        wmod = state[:, 0, BATCH:BATCH + 6 * DM]
        y2 = sb("y2", [P, 2, ND, CT])
        x_res = sb("x_res", [P, TT, DM])
        att = sb("att", [P, CT])
        x1 = sb("x1", [P, TT, DM])
        stats2 = sb("stats2", [P, TT, 6])
        mv2 = sb("mv2", [P, TT, 2])
        var2 = sb("var2", [P, TT])
        newton2 = sb("newton2", [P, TT])
        rstd2 = sb("rstd2", [P, TT])
        shift2 = sb("shift2", [P, TT])
        xn2 = sb("xn2", [P, TT, DM])
        h2T = sb("h2T", [P, CT])
        logits = sb("logits", [P, TT, NE])
        top = sb("top", [P, TT, 8])
        top_i = sb("top_i", [P, TT, 8], U32)
        top_f = sb("top_f", [P, TT, 2])
        gap = sb("gap", [P, TT, 1])
        gap_e = sb("gap_e", [P, TT, 1])
        gate = sb("gate", [P, TT, 3])
        pick = sb("pick", [P, 2, TT, NE])
        wexp = sb("wexp", [P, TT, NE])
        g = sb("g", [P, GB, KF, CT])
        acc = sb("acc", [P, TT, DM])
        out_t = sb("out_t", [P, TT, DM])

        ps_c = [pb("ps_c0"), pb("ps_c1")]
        ps_y = [pb("ps_y0"), pb("ps_y1")]
        stage, stage2 = pb("stage"), pb("stage2")
        pair = [stage, stage2]
        ps_h = pb("ps_h")
        ps_o = pb("ps_o")

        def seqs(buf, r):
            return buf[:, r, :].rearrange("p (k b t) -> p k b t", k=ND, b=CB)[:, :, :, 0:SEQ]

        modpack_loaded = sem("modpack_loaded")
        w_early, w_late = sem("w_early"), sem("w_late")
        x_in_loaded, x_res_loaded, stored = sem("x_in_loaded"), sem("x_res_loaded"), sem("stored")
        silu_c_done, mod_full, mods_s = sem("silu_c_done"), sem("mod_full"), sem("mods_s")
        gb_full, gb_s, gb_fix = sem("gb_full"), sem("gb_s"), sem("gb_fix")
        zeroed, pool_zeroed, a_exp, a_neg, sel_done = (sem("zeroed"), sem("pool_zeroed"), sem("a_exp"), sem("a_neg"),
                                                       sem("sel_done"))
        ln1_s, xn_done, ln1_full, hT_done = sem("ln1_s"), sem("xn_done"), sem("ln1_full"), sem("hT_done")
        xi_full, xpad_done, tap0_done, conv_s = sem("xi_full"), sem("xpad_done"), sem("tap0_done"), sem("conv_s")
        z_full, z_copied, silu_s = sem("z_full"), sem("z_copied"), sem("silu_s")
        xd_full, cast_s, rest_done, split_s = sem("xd_full"), sem("cast_s"), sem("rest_done"), sem("split_s")
        dt_full, dt_act, expln_s, corr_done, delta_s = (sem("dt_full"), sem("dt_act"), sem("expln_s"),
                                                        sem("corr_done"), sem("delta_s"))
        b_loaded = [sem(f"b_loaded{r}") for r in range(RING)]
        b_rows_stored, c_full = sem("b_rows_stored"), sem("c_full")
        decay_done, drive_done, scan_done, hc_done, summed = (sem("decay_done"), sem("drive_done"), sem("scan_done"),
                                                              sem("hc_done"), sem("summed"))
        y_read, y2_done = sem("y_read"), sem("y2_done")
        out_full, att_done, attT_full, x1_done = sem("out_full"), sem("att_done"), sem("attT_full"), sem("x1_done")
        ln2_s, xn2_done, ln2_full, h2T_done = sem("ln2_s"), sem("xn2_done"), sem("ln2_full"), sem("h2T_done")
        router_full, logits_done, route_s, gap_done, gap_exp = (sem("router_full"), sem("logits_done"), sem("route_s"),
                                                                sem("gap_done"), sem("gap_exp"))
        h_full, gelu_done, o_full, comb_s, out_s = (sem("h_full"), sem("gelu_done"), sem("o_full"), sem("comb_s"),
                                                    sem("out_s"))
        wexp_done = sem("wexp_done")
        mid_done = sem("mid_done")
        half_set = sem("half_set")
        hidden_copied = sem("hidden_copied")
        seed1, seed2 = sem("seed1"), sem("seed2")

        def reader(bank, use, i):
            c = i - 1
            if use.startswith("ffn"):
                return hidden_copied, 2 * NE * c + 2 * int(use[3:]) + (1 if bank == "ps_h" else 2)
            if use == "xdB":
                return split_s, 2 * i + 2
            if use == "xdF":
                return split_s, 2 * i + 3
            if use == "out":
                return att_done, CB * (c + 1)
            if use == "attT":
                return x1_done, c + 1
            if use == "ln2T":
                return h2T_done, CB * (c + 1)
            if use == "router":
                return logits_done, c + 1
            if use == "ln1T":
                return hT_done, CB * (i + 2)
            q = 2 * i + 1 if "B" in use else 2 * i + 2
            k = int(use[-1])
            if use.startswith("xi"):
                return xpad_done, ND * q + k + 1
            if use.startswith("z"):
                return z_copied, ND * q + k + 1
            return dt_act, 2 * ND * q + 2 * (k + 1)

        def wait_bank(pe, bank, use, i, skip, before):
            order = [x for x in BANK_USES[bank] if x not in skip]
            k = order.index(use)
            s, v = reader(bank, order[k - 1], i) if k else before[bank]
            pe.wait_ge(s, v)

        block = ctx.enter_context(nc.Block())

        @block.sync
        def _(sp):
            def load_x_in(c):
                sp.dma_start(x_in[:].rearrange("p s d -> p (s d)"), x_l[c]).then_inc(x_in_loaded, 16)

            def load_x_res(c):
                sp.dma_start(x_res[:].rearrange("p s d -> p (s d)"), x_l[c]).then_inc(x_res_loaded, 16)

            def store(c):
                sp.wait_ge(out_s, 2 * (c + 1))
                sp.dma_start(out_l[c], out_t[:].rearrange("p s d -> p (s d)")).then_inc(stored, 16)

            sp.dma_start(state[:, 0, 0:BATCH + 6 * DM], modpack).then_inc(modpack_loaded, 16)
            def store_b_rows(q, d):
                sp.wait_ge(cast_s, 2 * q + 1)
                sp.dma_start(b_rows[d], xdbl[0:NS, :]).then_inc(b_rows_stored, 16)

            def load_b(t, q, d, n, head, last):
                if n == NS - 1:
                    if not last:
                        sp.wait_ge(b_rows_stored, 16 * (q + 2))
                elif n == NS - 2:
                    sp.wait_ge(drive_done, t - RING + 2)
                elif head >= RING:
                    sp.wait_ge(drive_done, t - RING + 1)
                sp.dma_start(b_sb[:, n % RING, :], b_rows[d, n:n + 1, :].to_broadcast([P, CT])
                             ).then_inc(b_loaded[n % RING], 16)

            def iteration(i, first=False, after=True, before=True, ends=True):
                for s in range(NSTEP):
                    load_b(NSTEP * i + s, 2 * i + s // NS, s // NS, s % NS, s if first else RING,
                           last=(not before and s == NSTEP - 1))
                    if s == 1 and before:
                        sp.wait_ge(xn_done, TT * (i + 1))
                        load_x_in(i + 1)
                    elif s == 6 and ends:
                        store(i - 2)
                    elif s == 10:
                        store_b_rows(2 * i + 1, 1)
                    elif s == 15:
                        if after:
                            sp.wait_ge(x1_done, i)
                        load_x_res(i)
                    elif s == 26 and before:
                        store_b_rows(2 * i + 2, 0)

            load_x_in(0)
            sp.dma_start(wt[:, 0:EARLY], wpack[:, 0:EARLY]).then_inc(w_early, 16)
            sp.dma_start(wt[:, EARLY:NW], wpack[:, EARLY:NW]).then_inc(w_late, 16)
            store_b_rows(0, 0)
            sp.wait_ge(b_rows_stored, 16)
            iteration(0, first=True, after=False, ends=False)
            iteration(1, ends=False)
            with sp.Fori(2, NCH - 1) as i:
                iteration(i)
            iteration(NCH - 1, before=False)
            store(NCH - 2)
            store(NCH - 1)
            sp.wait_ge(stored, 16 * NCH)
            sp.wait_ge(b_rows_stored, 16 * 2 * NCH)

        @block.tensor
        def _(pe):
            def transpose_tiles(dst, src):
                for s in range(TT):
                    last = nc.tensor.transpose(dst[:, s * P:(s + 1) * P], src[:, s * P:(s + 1) * P], ident)
                return last

            def ln1T(c):
                pe.wait_ge(xn_done, TT * (c + 1))
                transpose_tiles(stage2, xn[:].rearrange("p s d -> p (s d)")).then_inc(ln1_full, 1)

            def xi(q, d, k, c):
                pe.wait_ge(hT_done, CB * (c + 1))
                nc.tensor.matmul(pair[k][:], inw[:, d, k * P:(k + 1) * P], hT[:], start=True, stop=True).then_inc(xi_full, 1)

            def zz(q, d, k):
                nc.tensor.matmul(pair[k][:], inw[:, d, DI + k * P:DI + (k + 1) * P], hT[:],
                                 start=True, stop=True).then_inc(z_full, 1)

            def xd(q, d):
                pe.wait_ge(silu_s, 2 * q + 2)
                for k in range(ND):
                    last = nc.tensor.matmul(ps_h[:], xpw[:, d, k, :], u[:, d, k, :], start=(k == 0), stop=(k == ND - 1))
                last.then_inc(xd_full, 1)

            def dt(q, d, k):
                pe.wait_ge(cast_s, 2 * q + 1)
                nc.tensor.matmul(pair[k][:], dtw[32:32 + DTR, d, k * P:(k + 1) * P], xdbl[32:32 + DTR, :],
                                 start=True, stop=True).then_inc(dt_full, 1)

            def bcast_c(t, q, d, n, first=False):
                if n == 0:
                    pe.wait_ge(split_s, q + 1)
                if not first:
                    pe.wait_ge(hc_done, t - 1)
                nc.tensor.matmul(ps_c[n % 2][:], selector[:, NS + n, :], parts[:, d, :],
                                 start=True, stop=True).then_inc(c_full, 1)

            def nsum(t, q, n, first=False):
                pe.wait_ge(hc_done, t + 1)
                if n == 0 and not first:
                    pe.wait_ge(y_read, ND * q)
                for k in range(ND):
                    last = nc.tensor.matmul(ps_y[k][:], ident, hc[:, n % 2, k, :], start=(n == 0), stop=(n == NS - 1))
                last.then_inc(summed, 1)

            def outproj(c):
                pe.wait_ge(y2_done, 2 * (c + 1))
                for j in range(2 * ND):
                    d, k = j // ND, j % ND
                    last = nc.tensor.matmul(stage[:], outw[:, d, k, :], y2[:, d, k, :], start=(j == 0), stop=(j == 2 * ND - 1))
                last.then_inc(out_full, 1)

            def attT(c):
                pe.wait_ge(att_done, CB * (c + 1))
                transpose_tiles(stage2, att).then_inc(attT_full, 1)

            def ln2T(c):
                pe.wait_ge(xn2_done, TT * (c + 1))
                transpose_tiles(stage, xn2[:].rearrange("p s d -> p (s d)")).then_inc(ln2_full, 1)

            def router(c):
                pe.wait_ge(h2T_done, CB * (c + 1))
                for s in range(TT):
                    last = nc.tensor.matmul(stage2[:, s * NE:(s + 1) * NE], h2T[:, s * P:(s + 1) * P], rw,
                                            start=True, stop=True)
                last.then_inc(router_full, 1)

            def hidden0(c, e):
                nc.tensor.matmul(ps_h[:], w1[:, e, 0:P], h2T[:], start=True, stop=True).then_inc(h_full, 1)

            def hidden1(c, e):
                nc.tensor.matmul(stage[:], w1[:, e, P:2 * P], h2T[:], start=True, stop=True).then_inc(h_full, 1)

            def expert_out(c, e, first=False):
                pe.wait_ge(gelu_done, NE * c + e + 1)
                if not first:
                    pe.wait_ge(comb_s, NE * TT * c + TT * e)
                for s in range(TT):
                    for k in range(KF):
                        last = nc.tensor.matmul(ps_o[:, s * DM:(s + 1) * DM], g[:, e % GB, k, s * P:(s + 1) * P],
                                                w2[:, e, k, :], start=(k == 0), stop=(k == KF - 1))
                last.then_inc(o_full, 1)

            def side(use, i, skip, before):
                c = i - 1
                if use.startswith("eo"):
                    e = int(use[2:])
                    expert_out(c, e, first=(e == 0 and isinstance(i, int) and i == 1))
                    return
                if use.startswith("xd"):
                    wait_bank(pe, "ps_h", use, i, skip, before)
                    xd(2 * i + (1 if use == "xdB" else 2), 1 if use == "xdB" else 0)
                    return
                if use.startswith("ffn"):
                    wait_bank(pe, "ps_h", use, i, skip, before)
                    hidden0(c, int(use[3:]))
                wait_bank(pe, "stage" if use in BANK_USES["stage"] else "stage2", use, i, skip, before)
                if use == "out":
                    outproj(c)
                elif use == "attT":
                    attT(c)
                elif use == "ln2T":
                    ln2T(c)
                elif use == "router":
                    router(c)
                elif use.startswith("ffn"):
                    hidden1(c, int(use[3:]))
                elif use == "ln1T":
                    ln1T(i + 1)
                else:
                    back = "B" in use
                    d, q, cc = (1, 2 * i + 1, i) if back else (0, 2 * i + 2, i + 1)
                    k = int(use[-1])
                    if use.startswith("xi"):
                        xi(q, d, k, cc)
                    elif use.startswith("z"):
                        zz(q, d, k)
                    else:
                        dt(q, d, k)

            PE_SIDE = {0: ["xiB0", "xiB1"], 1: ["zB0", "zB1"], 3: ["out"], 4: ["xdB"], 5: ["attT", "dtB0"], 6: ["dtB1"],
                       9: ["ln2T"], 10: ["router", "ffn0"], 11: ["ffn1"], 12: ["ffn2"], 13: ["ffn3", "ln1T"],
                       14: ["xiF0", "xiF1"], 18: ["eo0", "zF0", "zF1"], 19: ["ffn4"], 20: ["eo1", "xdF"],
                       21: ["dtF0", "dtF1"], 22: ["eo2", "ffn5"], 23: ["eo3", "ffn6"], 24: ["ffn7"],
                       26: ["eo4"], 27: ["eo5"], 28: ["eo6"], 29: ["eo7"]}

            def iteration(i, before, skip=(), first=False, last=False):
                q0 = 2 * i
                if first:
                    bcast_c(0, 0, 0, 0, first=True)
                for s in range(NSTEP):
                    t = NSTEP * i + s
                    if not (last and s == NSTEP - 1):
                        bcast_c(t + 1, q0 + (s + 1) // NS, ((s + 1) // NS) % 2, (s + 1) % NS, first=(first and s == 0))
                    if s > 0:
                        nsum(t - 1, q0 + (s - 1) // NS, (s - 1) % NS, first=(first and s == 1))
                    elif not first:
                        nsum(t - 1, q0 - 1, NS - 1)
                    for use in PE_SIDE.get(s, []):
                        if use not in skip:
                            side(use, i, skip, before)

            pe.wait_ge(silu_c_done, 1)
            for j in range(6):
                last = nc.tensor.matmul(stage[:, j * BATCH:(j + 1) * BATCH],
                                        wmod[:, j * DM:(j + 1) * DM], silu_c[:], start=True, stop=True)
            last.then_inc(mod_full, 1)
            for r in range(BATCH // 4):
                if r:
                    pe.wait_ge(gb_s, r)
                for j in range(4):
                    b = 4 * r + j
                    last = nc.tensor.matmul(ps_h[:, j * DM:(j + 1) * DM], silu_c[:, b:b + 1].to_broadcast([P, P]),
                                            wmod[:, 5 * DM:6 * DM], start=True, stop=True)
                last.then_inc(gb_full, 1)
            pe.wait_ge(gb_s, BATCH // 4)
            pe.wait_ge(w_early, 16)
            pe.wait_ge(mods_s, 1)
            for use in BEFORE_F:
                side(use, -1, [x for x in EVERY_USE if x not in BEFORE_F],
                     {"stage": (mods_s, 1), "stage2": (mods_s, 1), "ps_h": (gb_s, BATCH // 4)})
            pe.wait_ge(sel_done, 1)
            pe.wait_ge(w_late, 16)

            def last_uses(i, skip=()):
                return {bank: reader(bank, [x for x in uses if x not in skip][-1], i) for bank, uses in BANK_USES.items()}

            iteration(0, last_uses(-1, AFTER), skip=AFTER + [f"eo{e}" for e in range(NE)], first=True)
            iteration(1, last_uses(0, AFTER))
            with pe.Fori(2, NCH - 1) as i:
                iteration(i, last_uses(i - 1))
            iteration(NCH - 1, last_uses(NCH - 2), skip=BEFORE_F, last=True)
            nsum(NSTEP * NCH - 1, 2 * NCH - 1, NS - 1)
            for use in AFTER:
                if use == f"ffn{GB}":
                    for e in range(GB):
                        expert_out(NCH - 1, e)
                side(use, NCH, [x for x in EVERY_USE if x not in AFTER], last_uses(NCH - 1, BEFORE_F))
            for e in range(GB, NE):
                expert_out(NCH - 1, e)

        @block.scalar
        def _(act):
            def xn1(c):
                act.wait_ge(ln1_s, NORM * (c + 1))
                for s in range(TT):
                    nc.scalar.activation(xn[:, s, :], x_in[:, s, :], ACT.Identity, scale=rstd[:, s:s + 1],
                                         bias=shift[:, s:s + 1]).then_inc(xn_done, 1)

            def modulate1(c):
                act.wait_ge(ln1_full, c + 1)
                for b in range(CB):
                    nc.scalar.activation(hT[:, b * SEQ:(b + 1) * SEQ], stage2[:, b * SEQ:(b + 1) * SEQ], ACT.Identity,
                                         scale=mods[:, 1, bass.ds(CB * c + b, 1)],
                                         bias=mods[:, 0, bass.ds(CB * c + b, 1)]).then_inc(hT_done, 1)

            def xpad_copy(q, d, k):
                act.wait_ge(xi_full, ND * q + k + 1)
                at = (TAPS - 1) if d == 0 else 0
                nc.scalar.copy(xpad[:, d, k, :, at:at + SEQ],
                               pair[k][:].rearrange("p (b t) -> p b t", b=CB)).then_inc(xpad_done, 1)

            def tap0(q, d, k, first=False):
                act.wait_ge(xpad_done, ND * q + k + 1)
                if k == 0 and not first:
                    act.wait_ge(delta_s, DPARTS * (q - 1) + 1)
                at = 0 if d == 0 else TAPS - 1
                nc.scalar.activation(xc[:, k, :].rearrange("p (b t) -> p b t", b=CB), xpad[:, d, k, :, at:at + SEQ],
                                     ACT.Identity, scale=convw[:, d, k, 0:1], bias=convb[:, d, k:k + 1]
                                     ).then_inc(tap0_done, 1)

            def z_copy(q, d, k, first=False):
                act.wait_ge(z_full, ND * q + k + 1)
                if not first:
                    act.wait_ge(y2_done, q - 1)
                nc.scalar.copy(sz[:, d, k, :], pair[k][:]).then_inc(z_copied, 1)

            def silus(q, d):
                act.wait_ge(z_copied, ND * (q + 1))
                nc.scalar.activation(sz[:, d], sz[:, d], ACT.Silu).then_inc(silu_s, 1)
                act.wait_ge(conv_s, ND * (TAPS - 1) * (q + 1))
                nc.scalar.activation(u[:, d], xc[:], ACT.Silu).then_inc(silu_s, 1)

            def casts(q, d):
                act.wait_ge(xd_full, q + 1)
                if not (isinstance(q, int) and q == 0):
                    act.wait_ge(b_rows_stored, 16 * q)
                nc.scalar.copy(xdbl[0:64, :], ps_h[0:64, :]).then_inc(cast_s, 1)
                nc.scalar.copy(parts[:, d, :], ps_h[:]).then_inc(cast_s, 1)

            def dt_acts(q, d, k, first=False):
                act.wait_ge(dt_full, ND * q + k + 1)
                if k == 0 and not first:
                    act.wait_ge(delta_s, DPARTS * (q - 1) + 2)
                nc.scalar.activation(sp_e[:, k, :], pair[k][:], ACT.Abs, bias=dtb[:, d, k:k + 1]).then_inc(dt_act, 1)
                nc.scalar.activation(sp_r[:, k, :], pair[k][:], ACT.Relu, bias=dtb[:, d, k:k + 1]).then_inc(dt_act, 1)

            def exp_ln(q):
                act.wait_ge(dt_act, 2 * ND * (q + 1))
                nc.scalar.activation(sp_e[:], sp_e[:], ACT.Exp, scale=-1.0).then_inc(expln_s, 1)
                act.wait_ge(expln_s, 3 * q + 1)
                nc.scalar.activation(xc[:], sp_e[:], ACT.Identity, bias=1.0).then_inc(expln_s, 1)
                act.wait_ge(expln_s, 3 * q + 2)
                nc.scalar.activation(sp_l[:], xc[:], ACT.Ln).then_inc(expln_s, 1)

            def step(t, q, d, n, head):
                r = n % RING
                if n == 0:
                    act.wait_ge(delta_s, DPARTS * q + 2)
                if head >= RING:
                    act.wait_ge(scan_done, t - RING + 1)
                else:
                    act.wait_ge(zeroed, 1)
                for k in range(ND):
                    nc.scalar.activation(seqs(decay, r)[:, k], delta[:, d, k, :].rearrange("p (b t) -> p b t", b=CB),
                                         ACT.Exp, scale=amat[:, d, k, n:n + 1]).then_inc(decay_done, 1)

            def att_scale(c):
                act.wait_ge(out_full, c + 1)
                for b in range(CB):
                    nc.scalar.activation(att[:, b * SEQ:(b + 1) * SEQ], stage[:, b * SEQ:(b + 1) * SEQ], ACT.Identity,
                                         scale=mods[:, 2, bass.ds(CB * c + b, 1)]).then_inc(att_done, 1)

            def xn2_(c):
                act.wait_ge(ln2_s, NORM * (c + 1))
                for s in range(TT):
                    nc.scalar.activation(xn2[:, s, :], x1[:, s, :], ACT.Identity, scale=rstd2[:, s:s + 1],
                                         bias=shift2[:, s:s + 1]).then_inc(xn2_done, 1)

            def modulate2(c):
                act.wait_ge(ln2_full, c + 1)
                for b in range(CB):
                    nc.scalar.activation(h2T[:, b * SEQ:(b + 1) * SEQ], stage[:, b * SEQ:(b + 1) * SEQ], ACT.Identity,
                                         scale=mods[:, 4, bass.ds(CB * c + b, 1)],
                                         bias=mods[:, 3, bass.ds(CB * c + b, 1)]).then_inc(h2T_done, 1)

            def gate_exp(c):
                act.wait_ge(gap_done, c + 1)
                nc.scalar.activation(gap_e[:], gap[:], ACT.Exp).then_inc(gap_exp, 1)

            def hidden_copy(c, e, head=False):
                for k in range(KF):
                    act.wait_ge(h_full, 2 * NE * c + 2 * e + k + 1)
                    if k == 0 and not head:
                        act.wait_ge(o_full, NE * c + e - GB + 1)
                    nc.scalar.copy(g[:, e % GB, k, :], (ps_h if k == 0 else stage)[:]).then_inc(hidden_copied, 1)

            def gelus(c, e0):
                act.wait_ge(hidden_copied, 2 * NE * c + 2 * (e0 + GB))
                for e in range(e0, e0 + GB):
                    nc.scalar.activation(g[:, e % GB], g[:, e % GB], ACT.Gelu).then_inc(gelu_done, 1)

            def side(s, i, after=True, before=True, first=False, second=False):
                c = i - 1
                qb, qf = 2 * i + 1, 2 * i + 2
                if s == 0:
                    xpad_copy(qb, 1, 0)
                elif s == 1:
                    xpad_copy(qb, 1, 1)
                    tap0(qb, 1, 0)
                    tap0(qb, 1, 1)
                elif s == 3:
                    z_copy(qb, 1, 0, first)
                    z_copy(qb, 1, 1, first)
                elif s == 4:
                    silus(qb, 1)
                elif s == 5:
                    if after:
                        att_scale(c)
                    casts(qb, 1)
                elif s == 6:
                    dt_acts(qb, 1, 0)
                elif s == 7:
                    dt_acts(qb, 1, 1)
                    exp_ln(qb)
                elif s == 9 and after:
                    xn2_(c)
                elif s == 10 and after:
                    modulate2(c)
                elif s == 11 and after:
                    hidden_copy(c, 0, second)
                elif s == 12 and after:
                    hidden_copy(c, 1, second)
                elif s == 13:
                    if after:
                        hidden_copy(c, 2, second)
                        gate_exp(c)
                    if before:
                        xn1(i + 1)
                elif s == 14:
                    if after:
                        hidden_copy(c, 3, second)
                    if before:
                        modulate1(i + 1)
                elif s == 15 and after:
                    gelus(c, 0)
                elif s == 16 and before:
                    xpad_copy(qf, 0, 0)
                    xpad_copy(qf, 0, 1)
                    tap0(qf, 0, 0)
                    tap0(qf, 0, 1)
                elif s == 19 and before:
                    z_copy(qf, 0, 0)
                    z_copy(qf, 0, 1)
                elif s == 20:
                    if before:
                        silus(qf, 0)
                    if after:
                        hidden_copy(c, 4)
                elif s == 21 and before:
                    casts(qf, 0)
                elif s == 22 and before:
                    dt_acts(qf, 0, 0)
                    dt_acts(qf, 0, 1)
                elif s == 23:
                    if before:
                        exp_ln(qf)
                    if after:
                        hidden_copy(c, 5)
                elif s == 24 and after:
                    hidden_copy(c, 6)
                elif s == 25 and after:
                    hidden_copy(c, 7)
                elif s == 26 and after:
                    gelus(c, GB)

            def iteration(i, first=False, **kw):
                for s in range(NSTEP):
                    step(NSTEP * i + s, 2 * i + s // NS, s // NS, s % NS, s if first else RING)
                    side(s - LEAD, i, first=first, **kw)

            act.wait_ge(modpack_loaded, 16)
            nc.scalar.activation(silu_c[:], ct, ACT.Silu).then_inc(silu_c_done, 1)
            act.wait_ge(w_early, 16)
            act.wait_ge(mod_full, 1)
            nc.scalar.copy(mods[:].rearrange("p j b -> p (j b)"), stage[:, 0:6 * BATCH]).then_inc(mods_s, 1)
            for r in range(BATCH // 4):
                act.wait_ge(gb_full, r + 1)
                nc.scalar.copy(gb_rows[:, 4 * r:4 * r + 4, :].rearrange("p b d -> p (b d)"), ps_h[:]).then_inc(gb_s, 1)
            xn1(0)
            act.wait_ge(mods_s, 6)
            modulate1(0)
            act.wait_ge(pool_zeroed, 1)
            xpad_copy(0, 0, 0)
            xpad_copy(0, 0, 1)
            tap0(0, 0, 0, True)
            tap0(0, 0, 1)
            z_copy(0, 0, 0, True)
            z_copy(0, 0, 1, True)
            silus(0, 0)
            nc.scalar.activation(amat[:].rearrange("p r k n -> p (r k n)"), field("alog"), ACT.Exp).then_inc(a_exp, 1)
            casts(0, 0)
            dt_acts(0, 0, 0, True)
            dt_acts(0, 0, 1)
            exp_ln(0)
            act.wait_ge(a_neg, 1)
            iteration(0, first=True, after=False)
            iteration(1, second=True)
            with act.Fori(2, NCH - 1) as i:
                iteration(i)
            iteration(NCH - 1, before=False)
            c = NCH - 1
            att_scale(c)
            xn2_(c)
            modulate2(c)
            gate_exp(c)
            for e0 in (0, GB):
                for e in range(e0, e0 + GB):
                    hidden_copy(c, e)
                gelus(c, e0)

        @block.vector
        def _(dve):
            def norm_stats(src, st, m, v, s_, hold, c):
                for s in range(TT):
                    nc.vector.bn_stats(st[:, s, :], src[:, s, :]).then_inc(s_, 1)
                dve.wait_ge(s_, NORM * c + TT)
                nc.vector.memset(held[0:1, hold:hold + 1], 0.0)
                for s in range(TT):
                    nc.vector.bn_aggr(m[:, s, :], st[:, s, :]).then_inc(s_, 1)
                dve.wait_ge(s_, NORM * c + 2 * TT)
                nc.vector.tensor_scalar(v[:], m[:, :, 1], EPS, None, ALU.add).then_inc(s_, 1)

            def norm_root(m, v, rs, tmp, sh, s_, seed_done, c):
                n0 = NORM * c + 2 * TT + 1
                dve.wait_ge(seed_done, c + 1)
                nc.vector.tensor_tensor(tmp[:], rs[:], rs[:], ALU.mult).then_inc(s_, 1)
                dve.wait_ge(s_, n0 + 1)
                nc.vector.tensor_tensor(tmp[:], tmp[:], v[:], ALU.mult).then_inc(s_, 1)
                dve.wait_ge(s_, n0 + 2)
                nc.vector.tensor_scalar(tmp[:], tmp[:], -0.5, 1.5, ALU.mult, ALU.add).then_inc(s_, 1)
                dve.wait_ge(s_, n0 + 3)
                nc.vector.tensor_tensor(rs[:], rs[:], tmp[:], ALU.mult).then_inc(s_, 1)
                dve.wait_ge(s_, n0 + 4)
                nc.vector.scalar_tensor_tensor(out=sh[:], in0=m[:, :, 0], scalar=-1.0, in1=rs[:], op0=ALU.mult,
                                               op1=ALU.mult).then_inc(s_, 1)

            def ln1(c, first=False):
                dve.wait_ge(x_in_loaded, 16 * (c + 1))
                if not first:
                    dve.wait_ge(xn_done, TT * c)
                norm_stats(x_in, stats, mv, var, ln1_s, 0, c)

            def ln1_root(c):
                norm_root(mv, var, rstd, newton, shift, ln1_s, seed1, c)

            def taps(q, d, k):
                v = xc[:, k, :].rearrange("p (b t) -> p b t", b=CB)
                for j in range(1, TAPS):
                    if j == 1:
                        dve.wait_ge(tap0_done, ND * q + k + 1)
                    else:
                        dve.wait_ge(conv_s, (TAPS - 1) * (ND * q + k) + j - 1)
                    at = j if d == 0 else TAPS - 1 - j
                    nc.vector.scalar_tensor_tensor(out=v, in0=xpad[:, d, k, :, at:at + SEQ],
                                                   scalar=convw[:, d, k, j:j + 1], in1=v, op0=ALU.mult,
                                                   op1=ALU.add).then_inc(conv_s, 1)

            def residue(q, d):
                dve.wait_ge(cast_s, 2 * (q + 1))
                nc.vector.tensor_tensor(rest[64:128, :], ps_h[64:128, :], parts[64:128, d, :],
                                        ALU.subtract).then_inc(rest_done, 1)
                dve.wait_ge(rest_done, q + 1)
                nc.vector.tensor_copy(parts[64:128, d, :], rest[64:128, :]).then_inc(mid_done, 1)
                dve.wait_ge(mid_done, q + 1)
                nc.vector.tensor_tensor(parts[96:128, d, :], rest[96:128, :], parts[96:128, d, :],
                                        ALU.subtract).then_inc(split_s, 1)

            def correction(q):
                dve.wait_ge(expln_s, 3 * q + 2)
                nc.vector.scalar_tensor_tensor(out=sp_e[:], in0=xc[:], scalar=-1.0, in1=sp_e[:], op0=ALU.add,
                                               op1=ALU.subtract).then_inc(corr_done, 1)

            def scan(t, q, d, n, head):
                r = n % RING
                dve.wait_ge(decay_done, ND * (t + 1))
                dve.wait_ge(drive_done, t + 1)
                if head >= 2:
                    dve.wait_ge(hc_done, t - 1)
                rng = slice(None, None, -1) if d else slice(None)
                nc.vector.tensor_tensor_scan(state[:, n % 2, 0:WP - 1][:, rng], decay[:, r, 0:WP - 1][:, rng],
                                             drive[:, r, 0:WP - 1][:, rng], 0.0, ALU.mult, ALU.add).then_inc(scan_done, 1)

            def times_c(t, n, head):
                dve.wait_ge(scan_done, t + 1)
                dve.wait_ge(c_full, t + 1)
                if head >= 2:
                    dve.wait_ge(summed, t - 1)
                nc.vector.tensor_tensor(hc[:, n % 2].rearrange("p k (b t) -> p k b t", b=CB), seqs(state, n % 2),
                                        ps_c[n % 2][:].rearrange("p (b t) -> p b t", b=CB).unsqueeze(1)
                                        .to_broadcast([P, ND, CB, SEQ]), ALU.mult).then_inc(hc_done, 1)

            def residual(c):
                dve.wait_ge(attT_full, c + 1)
                dve.wait_ge(x_res_loaded, 16 * (c + 1))
                if not (isinstance(c, int) and c == 0):
                    dve.wait_ge(out_s, 2 * c)
                nc.vector.tensor_tensor(x1[:].rearrange("p s d -> p (s d)"), stage2[:],
                                        x_res[:].rearrange("p s d -> p (s d)"), ALU.add).then_inc(x1_done, 1)

            def ln2(c):
                dve.wait_ge(x1_done, c + 1)
                norm_stats(x1, stats2, mv2, var2, ln2_s, 1, c)

            def ln2_root(c):
                norm_root(mv2, var2, rstd2, newton2, shift2, ln2_s, seed2, c)

            def route_a(c):
                dve.wait_ge(router_full, c + 1)
                nc.vector.tensor_copy(logits[:].rearrange("p s e -> p (s e)"), stage2[:, 0:TT * NE]).then_inc(logits_done, 1)
                dve.wait_ge(logits_done, c + 1)
                nc.vector.memset(held[0:1, 2:3], 0.0)
                n0 = 2 * TT + 7
                for s in range(TT):
                    nc.vector.max(top[:, s, :], logits[:, s, :]).then_inc(route_s, 1)
                dve.wait_ge(route_s, n0 * c + TT)
                nc.vector.memset(held[0:1, 3:4], 0.0)
                for s in range(TT):
                    nc.vector.max_index(top_i[:, s, :], top[:, s, :], logits[:, s, :]).then_inc(route_s, 1)
                nc.vector.tensor_tensor(gap[:], top[:, :, 1:2], top[:, :, 0:1], ALU.subtract).then_inc(gap_done, 1)
                dve.wait_ge(route_s, n0 * c + 2 * TT)
                nc.vector.tensor_copy(top_f[:], top_i[:, :, 0:2]).then_inc(route_s, 1)

            def route_b(c):
                n0 = 2 * TT + 7
                k0 = n0 * c + 2 * TT + 1
                dve.wait_ge(gap_exp, c + 1)
                nc.vector.tensor_scalar(gate[:, :, 0:1], gap_e[:], 1.0, None, ALU.add).then_inc(route_s, 1)
                dve.wait_ge(route_s, k0 + 1)
                nc.vector.reciprocal(gate[:, :, 1:2], gate[:, :, 0:1]).then_inc(route_s, 1)
                dve.wait_ge(route_s, k0 + 2)
                nc.vector.tensor_tensor(gate[:, :, 2:3], gate[:, :, 1:2], gap_e[:], ALU.mult).then_inc(route_s, 1)
                for j in range(2):
                    nc.vector.tensor_tensor(pick[:, j], iota8.unsqueeze(1).to_broadcast([P, TT, NE]),
                                            top_f[:, :, j:j + 1].to_broadcast([P, TT, NE]), ALU.is_equal).then_inc(route_s, 1)
                dve.wait_ge(route_s, k0 + 5)
                nc.vector.tensor_tensor(pick[:].rearrange("p j s e -> p s j e"), pick[:].rearrange("p j s e -> p s j e"),
                                        gate[:, :, 1:3].unsqueeze(3).to_broadcast([P, TT, 2, NE]),
                                        ALU.mult).then_inc(route_s, 1)
                dve.wait_ge(route_s, k0 + 6)
                nc.vector.tensor_tensor(wexp[:], pick[:, 0], pick[:, 1], ALU.add).then_inc(wexp_done, 1)

            def combine(c, e):
                dve.wait_ge(o_full, NE * c + e + 1)
                if e == 0:
                    dve.wait_ge(wexp_done, c + 1)
                    if not (isinstance(c, int) and c == 0):
                        dve.wait_ge(out_s, 2 * c)
                else:
                    dve.wait_ge(comb_s, NE * TT * c + TT * e)
                for s in range(TT):
                    src = ps_o[:, s * DM:(s + 1) * DM]
                    if e == 0:
                        nc.vector.tensor_scalar(acc[:, s, :], src, wexp[:, s, 0:1], None, ALU.mult).then_inc(comb_s, 1)
                    else:
                        nc.vector.scalar_tensor_tensor(out=acc[:, s, :], in0=src, scalar=wexp[:, s, e:e + 1],
                                                       in1=acc[:, s, :], op0=ALU.mult, op1=ALU.add).then_inc(comb_s, 1)

            def side(s, i, after=True, before=True, first=False):
                c = i - 1
                qb, qf = 2 * i + 1, 2 * i + 2
                if s == 1 and after:
                    y_out_b(c)
                elif s == 2:
                    taps(qb, 1, 0)
                elif s == 3:
                    taps(qb, 1, 1)
                elif s == 6:
                    residue(qb, 1)
                elif s == 7 and after:
                    residual(c)
                    ln2(c)
                elif s == 8:
                    correction(qb)
                elif s == 9 and after:
                    ln2_root(c)
                elif s == 10 and before:
                    ln1(i + 1)
                elif s == 12 and after:
                    route_a(c)
                elif s == 13 and before:
                    ln1_root(i + 1)
                elif s == 14 and after:
                    route_b(c)
                elif s == 17:
                    y_out_f(i)
                elif s == 18 and before:
                    taps(qf, 0, 0)
                elif s == 19 and before:
                    taps(qf, 0, 1)
                elif s == 22 and before:
                    residue(qf, 0)
                elif s == 24 and before:
                    correction(qf)
                e = {20: 0, 21: 1, 23: 2, 25: 3, 27: 4, 28: 5, 29: 6, 30: 7}.get(s)
                if e is not None and after:
                    combine(c, e)

            def y_out_b(c):
                y_pass(2 * c + 1, 1, c)

            def y_out_f(c):
                y_pass(2 * c, 0, c)

            def y_pass(q, d, c):
                dve.wait_ge(summed, NS * (q + 1))
                if not (isinstance(c, int) and c == 0):
                    dve.wait_ge(out_full, c)
                for k in range(ND):
                    nc.vector.scalar_tensor_tensor(out=y2[:, d, k, :], in0=u[:, d, k, :], scalar=dp[:, d, k:k + 1],
                                                   in1=ps_y[k][:], op0=ALU.mult, op1=ALU.add).then_inc(y_read, 1)

            def iteration(i, first=False, **kw):
                for s in range(NSTEP):
                    t = NSTEP * i + s
                    scan(t, 2 * i + s // NS, s // NS, s % NS, s if first else RING)
                    if not (first and s == 0):
                        times_c(t - 1, (s - 1) % NS, s - 1 if first else RING)
                    side(s, i, first=first, **kw)

            ln1(0, first=True)
            ln1_root(0)
            nc.vector.memset(decay[:], 0.0)
            nc.vector.memset(drive[:], 0.0).then_inc(zeroed, 1)
            dve.wait_ge(mods_s, 1)
            nc.vector.tensor_scalar(mods[:, 1], mods[:, 1], 1.0, None, ALU.add).then_inc(mods_s, 1)
            nc.vector.tensor_scalar(mods[:, 4], mods[:, 4], 1.0, None, ALU.add).then_inc(mods_s, 1)
            nc.vector.scalar_tensor_tensor(out=mod_t[:, 0], in0=mods[:, 2], scalar=-1.0, in1=mods[:, 2], op0=ALU.mult,
                                           op1=ALU.max).then_inc(mods_s, 1)
            nc.vector.tensor_scalar(mod_t[:, 1], mods[:, 2], 0.0, 0.5, ALU.is_ge, ALU.subtract).then_inc(mods_s, 1)
            dve.wait_ge(mods_s, 5)
            nc.vector.scalar_tensor_tensor(out=mods[:, 2], in0=mod_t[:, 0], scalar=0.25, in1=mod_t[:, 1], op0=ALU.max,
                                           op1=ALU.mult).then_inc(mods_s, 1)
            dve.wait_ge(w_early, 16)
            nc.vector.tensor_copy(selector[:], field("sel32").unsqueeze(2).to_broadcast([P, 2 * NS, P])).then_inc(sel_done, 1)
            taps(0, 0, 0)
            taps(0, 0, 1)
            residue(0, 0)
            correction(0)
            dve.wait_ge(a_exp, 1)
            nc.vector.tensor_scalar(amat[:].rearrange("p r k n -> p (r k n)"),
                                    amat[:].rearrange("p r k n -> p (r k n)"), -1.0, None, ALU.mult).then_inc(a_neg, 1)
            dve.wait_ge(gb_s, BATCH // 4)
            hv = hc[:].rearrange("p a k t -> p (a k t)")
            gv = gb_rows[:].rearrange("p b d -> p (b d)")
            nc.vector.scalar_tensor_tensor(out=hv, in0=gv, scalar=-1.0, in1=gv, op0=ALU.mult, op1=ALU.max).then_inc(gb_fix, 1)
            dve.wait_ge(gb_fix, 1)
            nc.vector.tensor_scalar(gv, gv, 0.0, 0.5, ALU.is_ge, ALU.subtract).then_inc(gb_fix, 1)
            dve.wait_ge(gb_fix, 2)
            nc.vector.tensor_scalar(hv, hv, 0.25, 2.0, ALU.max, ALU.mult).then_inc(gb_fix, 1)
            dve.wait_ge(gb_fix, 3)
            nc.vector.tensor_tensor(gv, gv, hv, ALU.mult).then_inc(gb_fix, 1)
            dve.wait_ge(gb_fix, 4)
            iteration(0, first=True, after=False)
            iteration(1)
            with dve.Fori(2, NCH - 1) as i:
                iteration(i)
            iteration(NCH - 1, before=False)
            times_c(NSTEP * NCH - 1, NS - 1, RING)
            c = NCH - 1
            y_out_b(c)
            residual(c)
            ln2(c)
            ln2_root(c)
            route_a(c)
            route_b(c)
            for e in range(NE):
                combine(c, e)

        @block.gpsimd
        def _(pool):
            def root_seed(v, rs, s_, seed_done, used, c):
                pool.wait_ge(s_, NORM * c + 2 * TT + 1)
                if not (isinstance(c, int) and c == 0):
                    pool.wait_ge(used, TT * c)
                nc.gpsimd.tensor_tensor(rs[:], v[:], minus_half[:], ALU.pow).then_inc(seed_done, 1)

            def delta_part(q, d, part):
                if part == 0:
                    pool.wait_ge(expln_s, 3 * (q + 1))
                    pool.wait_ge(corr_done, q + 1)
                    nc.gpsimd.tensor_tensor(sp_l[:], sp_l[:], sp_e[:], ALU.subtract).then_inc(delta_s, 1)
                elif part == 1:
                    pool.wait_ge(delta_s, DPARTS * q + 1)
                    nc.gpsimd.tensor_tensor(delta[:, d], sp_l[:], sp_r[:], ALU.add).then_inc(delta_s, 1)
                else:
                    pool.wait_ge(delta_s, DPARTS * q + 2)
                    nc.gpsimd.tensor_tensor(du[:, d], delta[:, d], u[:, d], ALU.mult).then_inc(delta_s, 1)

            def drive_step(t, q, d, n, head):
                r = n % RING
                pool.wait_ge(b_loaded[r], 16 * (NS // RING * q + n // RING + 1))
                if n == 0:
                    pool.wait_ge(delta_s, DPARTS * (q + 1))
                if head >= RING:
                    pool.wait_ge(scan_done, t - RING + 1)
                else:
                    pool.wait_ge(zeroed, 1)
                nc.gpsimd.tensor_tensor(seqs(drive, r), du[:, d].rearrange("p k (b t) -> p k b t", b=CB),
                                        b_sb[:, r, :].rearrange("p (b t) -> p b t", b=CB).unsqueeze(1)
                                        .to_broadcast([P, ND, CB, SEQ]), ALU.mult).then_inc(drive_done, 1)

            def gate_y(q, d):
                pool.wait_ge(y_read, ND * (q + 1))
                nc.gpsimd.tensor_tensor(y2[:, d], y2[:, d], sz[:, d], ALU.mult).then_inc(y2_done, 1)

            def finish(c):
                pool.wait_ge(comb_s, NE * TT * (c + 1))
                if not (isinstance(c, int) and c == 0):
                    pool.wait_ge(stored, 16 * c)
                nc.gpsimd.tensor_tensor(out_t[:].rearrange("p (b s) d -> p b s d", b=CB),
                                        acc[:].rearrange("p (b s) d -> p b s d", b=CB),
                                        gb_rows[:, bass.ds(CB * c, CB), :].unsqueeze(2)
                                        .to_broadcast([P, CB, TT // CB, DM]), ALU.mult).then_inc(out_s, 1)
                pool.wait_ge(out_s, 2 * c + 1)
                nc.gpsimd.tensor_tensor(out_t[:], out_t[:], x1[:], ALU.add).then_inc(out_s, 1)

            def iteration(i, first=False, after=True, before=True, ends=True):
                for s in range(NSTEP):
                    drive_step(NSTEP * i + s, 2 * i + s // NS, s // NS, s % NS, s if first else RING)
                    if s == 2 and ends:
                        finish(i - 2)
                    if s == 5 and after:
                        gate_y(2 * i - 1, 1)
                    elif s == 10 and after:
                        root_seed(var2, rstd2, ln2_s, seed2, xn2_done, i - 1)
                    elif s in (12, 13, 14):
                        delta_part(2 * i + 1, 1, s - 12)
                    elif s == 15 and before:
                        root_seed(var, rstd, ln1_s, seed1, xn_done, i + 1)
                    elif s == 20:
                        gate_y(2 * i, 0)
                    elif s in (28, 29, 30) and before:
                        delta_part(2 * i + 2, 0, s - 28)

            nc.gpsimd.memset(minus_half[:], -0.5).then_inc(half_set, 1)
            nc.gpsimd.memset(xpad[:], 0.0).then_inc(pool_zeroed, 1)
            pool.wait_ge(half_set, 1)
            root_seed(var, rstd, ln1_s, seed1, xn_done, 0)
            for part in range(DPARTS):
                delta_part(0, 0, part)
            iteration(0, first=True, after=False, ends=False)
            iteration(1, ends=False)
            pool.wait_ge(gb_fix, 4)
            with pool.Fori(2, NCH - 1) as i:
                iteration(i)
            iteration(NCH - 1, before=False)
            finish(NCH - 2)
            gate_y(2 * NCH - 1, 1)
            root_seed(var2, rstd2, ln2_s, seed2, xn2_done, NCH - 1)
            finish(NCH - 1)


def kernel(**inputs):
    import numpy as np
    import concourse.bacc as bacc
    from concourse.bass_utils import run_bass_kernel_spmd as run

    a = {k: np.asarray(v) for k, v in inputs.items()}
    pack = np.zeros((P, NW), np.float32)

    def put(name, value):
        lo, hi = AT[name]
        pack[:, lo:hi] = value.reshape(P, hi - lo)

    def both(name):
        return [a[f"L0_attn_{name}_f"], a[f"L0_attn_{name}_b"]]

    def channels(v):
        return v.reshape(ND, P, -1).transpose(1, 0, 2)

    put("ident", np.eye(P, dtype=np.float32))
    sel = np.zeros((P, 32), np.float32)
    for base in (0, 64, 96):
        sel[base:base + 32] = np.eye(32, dtype=np.float32)
    put("sel32", sel)
    put("iota8", np.tile(np.arange(NE, dtype=np.float32), (P, 1)))
    put("inw", np.stack([v.T for v in both("inW")], 1))
    xp = np.zeros((P, 2, ND, P), np.float32)
    for d, v in enumerate(both("xpW")):
        cols = channels(v.T)
        for base in (0, 64, 96):
            xp[:, d, :, base:base + 2 * NS] = cols[:, :, DTR:]
        xp[:, d, :, 32:32 + DTR] = cols[:, :, :DTR]
    put("xpw", xp)
    dtw = np.zeros((P, 2, DI), np.float32)
    for d, v in enumerate(both("dtW")):
        dtw[32:32 + DTR, d] = v.T
    put("dtw", dtw)
    put("convw", np.stack([channels(v.reshape(DI, TAPS)) for v in both("convW")], 1))
    put("convb", np.stack([channels(v)[:, :, 0] for v in both("convB")], 1))
    put("dtb", np.stack([channels(v)[:, :, 0] for v in both("dtB")], 1))
    put("alog", np.stack([channels(v) for v in both("Alog")], 1))
    put("dp", np.stack([channels(v)[:, :, 0] for v in both("Dp")], 1))
    put("rw", a["L0_ffn_router_w"].T)
    put("outw", np.stack([channels(v.T) for v in both("outW")], 1))
    put("w1", a["L0_ffn_w1"].transpose(1, 0, 2))
    put("w2", a["L0_ffn_w2"].reshape(NE, KF, P, DM).transpose(2, 0, 1, 3))
    x_l = np.ascontiguousarray(a["L0_attn_x"].reshape(NCH, TT, P, DM).transpose(0, 2, 1, 3)).reshape(NCH, P, TT * DM)

    nc = bacc.Bacc("TRN2", target_bir_lowering=False, num_devices=1)
    arrays = {"x_l": x_l, "modpack": np.concatenate([a["L0_c"].T, a["L0_wmod"]], 1), "wpack": pack}
    args = [nc.dram_tensor(k, v.shape, mybir.dt.from_np(v.dtype), kind="ExternalInput").ap() for k, v in arrays.items()]
    args.append(nc.dram_tensor("b_rows", (2, NS, CT), F32, kind="Internal").ap())
    args.append(nc.dram_tensor("out_l", x_l.shape, F32, kind="ExternalOutput").ap())
    build(nc, *args)
    r = run(nc, [arrays], core_ids=[0])
    return np.asarray(r.results[0]["out_l"]).reshape(NCH, P, TT, DM).transpose(0, 2, 1, 3).reshape(BATCH, SEQ, DM)
```

```python
import concourse.bass as bass
from concourse import mybir
from contextlib import ExitStack

F32 = mybir.dt.float32
BF16 = mybir.dt.bfloat16
U32 = mybir.dt.uint32
ALU = mybir.AluOpType
ACT = mybir.ActivationFunctionType

P = 128
BATCH, SEQ, DM = 16, 256, 128
DI, NS, DTR, TAPS = 256, 16, 8, 4
ND = DI // P
NE, FH = 8, 256
KF = FH // P
CB = 2
CT = CB * SEQ
NCH = BATCH // CB
TT = CT // P
PAD = SEQ + 1
WP = ND * CB * PAD
NSTEP = 2 * NS
RING = 4
SB = 4
CRING = 2
CLAG = 3
HB = 4
MODS = 7
GATE_STEP = 13
LEAD = 3
DPARTS = 3
GB = 6
GS = 4
EPS = 1e-5
NORM = 2 * TT + 5

XR = 2 * NS + DTR

FIELDS = [("ident", P), ("iota8", NE),
          ("inw", 2 * 2 * DI), ("xpw", 2 * ND * XR), ("dtw", 2 * DI), ("convw", 2 * ND * TAPS), ("convb", 2 * ND),
          ("dtb", 2 * ND), ("alog", 2 * ND * NS), ("dp", 2 * ND), ("rw", NE),
          ("outw", 2 * ND * DM), ("w1", NE * FH), ("w2", NE * KF * DM)]
AT, NW = {}, 0
for _name, _n in FIELDS:
    AT[_name] = (NW, NW + _n)
    NW += _n
EARLY = AT["rw"][1]

PE_SIDE = {0: "xiB0 xiB1", 1: "zB0", 2: "zB1", 3: "out xdB attT", 4: "dtB0 ln1T dtB1", 6: "xiF0", 8: "xiF1",
           9: "ln2T", 10: "router ffn0", 11: "ffn1 ffn2", 12: "ffn3", 13: "ffn4", 14: "ffn5", 16: "zF0 zF1 eo0",
           18: "eo1", 19: "eo2 xdF", 20: "dtF0 dtF1 eo3", 22: "ffn6", 23: "ffn7", 27: "eo4 eo5 eo6", 28: "eo7"}
ACT_SIDE = {2: "centreB0 centreB1", 4: "siluB", 5: "att", 6: "xdB xn1 dtB0", 7: "dtB1 mod1 explnB xn2", 8: "mod2",
            9: "centreF0", 10: "hid0", 11: "hid1 centreF1", 12: "hid2", 13: "hid3", 14: "hid4", 15: "gapexp",
            16: "hid5 gelu0", 19: "siluF", 21: "xdF", 23: "dtF0 dtF1", 24: "explnF hid6", 27: "hid7 gelu1"}
DVE_SIDE = {0: "ln1", 1: "yB", 2: "tapB0", 3: "tapB1 tapB2", 5: "root1", 6: "res", 8: "root2", 10: "corrB",
            11: "routeA", 13: "tapF0", 14: "tapF1", 15: "tapF2", 16: "routeB", 17: "yF", 19: "comb0", 21: "comb1",
            22: "comb2", 24: "comb3", 25: "corrF", 29: "comb4", 30: "comb5", 31: "comb6 comb7"}
POOL_SIDE = {3: "seed1 finish", 4: "gateB", 8: "seed2", 13: "dB0 dB1", 15: "dB2", 20: "gateF", 29: "dF0", 30: "dF1",
             31: "dF2"}
SP_SIDE = {1: "x_in", 4: "store", 5: "x1", 9: "rowsB", 29: "rowsF"}
AFTER = ("out attT ln2T router ffn0 ffn1 ffn2 ffn3 ffn4 ffn5 ffn6 ffn7 eo0 eo1 eo2 eo3 eo4 eo5 eo6 eo7 att xn2 mod2 hid0 "
         "hid1 hid2 hid3 hid4 hid5 hid6 hid7 gapexp gelu0 gelu1 yB res root2 routeA routeB comb0 comb1 comb2 comb3 comb4 "
         "comb5 comb6 comb7 gateB seed2 x1").split()
NEXT = ("ln1T xiF0 xiF1 zF0 zF1 xdF dtF0 dtF1 xn1 mod1 centreF0 centreF1 siluF explnF ln1 root1 tapF0 tapF1 tapF2 corrF seed1 "
        "dF0 dF1 dF2 x_in rowsF").split()
FFN = [f"ffn{e}" for e in range(NE)]
BANK_OF = {"stage": ["xiB0", "out", "dtB0", "xiF0", "dtF0"],
           "stage2": ["xiB1", "attT", "dtB1", "xiF1", "dtF1"],
           "ps_h": ["zB0", "xdB", "ln2T", "zF0", "xdF"] + FFN,
           "ps_h1": ["zB1", "ln1T", "zF1"] + FFN}
PE_ORDER = [use for step in sorted(PE_SIDE) for use in PE_SIDE[step].split()]
BANK_USES = {bank: [use for use in PE_ORDER if use in uses] for bank, uses in BANK_OF.items()}
EVERY_USE = [use for uses in BANK_USES.values() for use in uses]


def build(nc, x_l, modpack, wpack, bc_rows, out_l):
    ctx = ExitStack()
    with ctx:
        def sb(name, shape, dt=F32):
            return ctx.enter_context(nc.sbuf_tensor(name, shape, dt))

        def pb(name, shape=(P, CT), dt=F32):
            return ctx.enter_context(nc.psum_tensor(name, list(shape), dt))

        def sem(name):
            return ctx.enter_context(nc.semaphore(name))

        wt = sb("wt", [P, NW])

        def field(name):
            return wt[:, AT[name][0]:AT[name][1]]

        ident = field("ident")
        iota8 = field("iota8")
        inw = field("inw").rearrange("p (r e) -> p r e", r=2)
        xpw = field("xpw").rearrange("p (r k m) -> p r k m", r=2, k=ND)
        dtw = field("dtw").rearrange("p (r e) -> p r e", r=2)
        convw = field("convw").rearrange("p (r k t) -> p r k t", r=2, k=ND)
        convb = field("convb").rearrange("p (r k) -> p r k", r=2)
        dtb = field("dtb").rearrange("p (r k) -> p r k", r=2)
        dp = field("dp").rearrange("p (r k) -> p r k", r=2)
        outw = field("outw").rearrange("p (r k o) -> p r k o", r=2, k=ND)
        rw = field("rw")
        w1 = field("w1").rearrange("p (e f) -> p e f", e=NE)
        w2 = field("w2").rearrange("p (e k d) -> p e k d", e=NE, k=KF)
        amat = sb("amat", [P, 2, ND, NS])
        silu_c = sb("silu_c", [P, BATCH])
        mods = sb("mods", [P, 6, BATCH])
        mod_t = sb("mod_t", [P, 2, 2, BATCH])
        gb_rows = sb("gb_rows", [P, BATCH, DM])
        minus_half = sb("minus_half", [P, TT])
        held = sb("held", [P, 4])

        x_in = sb("x_in", [P, TT, DM])
        stats = sb("stats", [P, TT, 6])
        mv = sb("mv", [P, TT, 2])
        var = sb("var", [P, TT])
        newton = sb("newton", [P, TT])
        rstd = sb("rstd", [P, TT])
        shift = sb("shift", [P, TT])
        xn = sb("xn", [P, TT, DM])
        hT = sb("hT", [P, CT])
        xc = sb("xc", [P, ND, CT])
        u = sb("u", [P, 2, ND, CT])
        sz = sb("sz", [P, 2, ND, CT])
        xdbl = sb("xdbl", [P, CT])
        sp_e = sb("sp_e", [P, ND, CT])
        sp_l = sb("sp_l", [P, ND, CT])
        sp_r = sb("sp_r", [P, ND, CT])
        delta = sb("delta", [P, 2, ND, CT])
        du = sb("du", [P, 2, ND, CT])
        b_sb = sb("b_sb", [P, RING, CT])
        c_sb = sb("c_sb", [P, CRING, CT])
        decay = sb("decay", [P, RING, WP])
        drive = sb("drive", [P, RING, WP])
        state = sb("state", [P, SB, WP])
        hc = sb("hc", [P, HB, ND, CT])
        y2 = sb("y2", [P, 2, ND, CT])
        x1 = sb("x1", [P, TT, DM])
        stats2 = sb("stats2", [P, TT, 6])
        mv2 = sb("mv2", [P, TT, 2])
        var2 = sb("var2", [P, TT])
        newton2 = sb("newton2", [P, TT])
        rstd2 = sb("rstd2", [P, TT])
        shift2 = sb("shift2", [P, TT])
        xn2 = xn
        h2T = sb("h2T", [P, CT])
        att = h2T
        logits = sb("logits", [P, TT, NE])
        top = sb("top", [P, TT, 8])
        top_i = sb("top_i", [P, TT, 8], U32)
        top_f = sb("top_f", [P, TT, 2])
        gap = sb("gap", [P, TT, 1])
        gap_e = sb("gap_e", [P, TT, 1])
        gate = sb("gate", [P, TT, 3])
        pick = sb("pick", [P, 2, TT, NE])
        wexp = sb("wexp", [P, TT, NE])
        g = sb("g", [P, GB, KF, CT])
        modpack_sb = state[:, 0, 0:BATCH + 6 * DM]
        ct, wmod = modpack_sb[:, 0:BATCH], modpack_sb[:, BATCH:]
        acc = sb("acc", [P, TT, DM])

        ps_y = [pb("ps_y0"), pb("ps_y1")]
        stage, stage2 = pb("stage"), pb("stage2")
        pair = [stage, stage2]
        ps_h = pb("ps_h")
        ps_h1 = pb("ps_h1")
        h_pair = [ps_h, ps_h1]
        ps_o = [pb("ps_o0"), pb("ps_o1")]

        def seqs(buf, r):
            return buf[:, r, :].rearrange("p (k b t) -> p k b t", k=ND, b=CB)[:, :, :, 0:SEQ]

        modpack_loaded = sem("modpack_loaded")
        w_early, w_late = sem("w_early"), sem("w_late")
        x_in_loaded, x1_loaded, stored = sem("x_in_loaded"), sem("x1_loaded"), sem("stored")
        silu_c_done, mod_full, mods_s = sem("silu_c_done"), sem("mod_full"), sem("mods_s")
        gb_full, gb_s = sem("gb_full"), sem("gb_s")
        zeroed, a_exp, a_neg = sem("zeroed"), sem("a_exp"), sem("a_neg")
        ln1_s, xn_done, ln1_full, hT_done = sem("ln1_s"), sem("xn_done"), sem("ln1_full"), sem("hT_done")
        xi_full, centre_done, conv_s, u_done = sem("xi_full"), sem("centre_done"), sem("conv_s"), sem("u_done")
        z_full, sz_done = sem("z_full"), sem("sz_done")
        xd_full, xdbl_done = sem("xd_full"), sem("xdbl_done")
        dt_full, dt_act, expln_s, corr_done, delta_s = (sem("dt_full"), sem("dt_act"), sem("expln_s"),
                                                        sem("corr_done"), sem("delta_s"))
        b_loaded = [sem(f"b_loaded{r}") for r in range(RING)]
        c_loaded = [sem(f"c_loaded{r}") for r in range(CRING)]
        rows_stored = sem("rows_stored")
        decay_done, drive_done, scan_done, hc_done, summed = (sem("decay_done"), sem("drive_done"), sem("scan_done"),
                                                              sem("hc_done"), sem("summed"))
        y_read, y2_done = sem("y_read"), sem("y2_done")
        out_full, att_done, attT_full, x1_done = sem("out_full"), sem("att_done"), sem("attT_full"), sem("x1_done")
        ln2_s, xn2_done, ln2_full, h2T_done = sem("ln2_s"), sem("xn2_done"), sem("ln2_full"), sem("h2T_done")
        router_full, logits_done, route_s, gap_done, gap_exp = (sem("router_full"), sem("logits_done"), sem("route_s"),
                                                                sem("gap_done"), sem("gap_exp"))
        h_full, gelu_done, o_full, comb_s, out_s = (sem("h_full"), sem("gelu_done"), sem("o_full"), sem("comb_s"),
                                                    sem("out_s"))
        wexp_done = sem("wexp_done")
        half_set = sem("half_set")
        hidden_copied = sem("hidden_copied")
        seed1, seed2 = sem("seed1"), sem("seed2")

        def reader(bank, use, i):
            c = i - 1
            if use.startswith("ffn"):
                return hidden_copied, 2 * NE * c + 2 * int(use[3:]) + (1 if bank == "ps_h" else 2)
            if use == "xdB":
                return xdbl_done, 2 * i + 2
            if use == "xdF":
                return xdbl_done, 2 * i + 3
            if use == "out":
                return att_done, CB * (c + 1)
            if use == "attT":
                return x1_done, c + 1
            if use == "ln2T":
                return h2T_done, CB * (c + 1)
            if use == "ln1T":
                return hT_done, CB * (i + 2)
            q = 2 * i + 1 if "B" in use else 2 * i + 2
            k = int(use[-1])
            if use.startswith("xi"):
                return conv_s, ND * (TAPS - 1) * (q + 1) - ND + k + 1
            if use.startswith("z"):
                return sz_done, ND * q + k + 1
            return dt_act, 2 * ND * q + 2 * (k + 1)

        def wait_bank(pe, bank, use, i, skip, before):
            order = [x for x in BANK_USES[bank] if x not in skip]
            k = order.index(use)
            last = reader(bank, order[k - 1], i) if k else before[bank]
            if last:
                pe.wait_ge(*last)

        block = ctx.enter_context(nc.Block())

        @block.sync
        def _(sp):
            def load_x_in(c):
                sp.dma_start(x_in[:].rearrange("p s d -> p (s d)"), x_l[c]).then_inc(x_in_loaded, 16)

            def load_x1(c):
                if not (isinstance(c, int) and c == 0):
                    sp.wait_ge(out_s, 2 * c)
                sp.dma_start(x1[:].rearrange("p s d -> p (s d)"), x_l[c]).then_inc(x1_loaded, 16)

            def store(c):
                sp.wait_ge(out_s, 2 * (c + 1))
                sp.dma_start(out_l[c], acc[:].rearrange("p s d -> p (s d)")).then_inc(stored, 16)

            def store_rows(q, d):
                sp.wait_ge(xdbl_done, q + 1)
                sp.dma_start(bc_rows[d], xdbl[0:2 * NS, :]).then_inc(rows_stored, 16)

            def load_b(t, q, d, n, head, last):
                if n == NS - 1:
                    if not last:
                        sp.wait_ge(rows_stored, 16 * (q + 2))
                elif n == NS - 2:
                    sp.wait_ge(drive_done, t - RING + 2)
                elif head >= RING:
                    sp.wait_ge(drive_done, t - RING + 1)
                sp.dma_start(b_sb[:, n % RING, :], bc_rows[d, n:n + 1, :].to_broadcast([P, CT])
                             ).then_inc(b_loaded[n % RING], 16)

            def load_c(t, d, n, head):
                if head >= CRING:
                    sp.wait_ge(hc_done, t - CRING + 1)
                sp.dma_start(c_sb[:, n % CRING, :], bc_rows[d, NS + n:NS + n + 1, :].to_broadcast([P, CT])
                             ).then_inc(c_loaded[n % CRING], 16)

            def iteration(i, first=False, after=True, before=True, ends=True):
                for s in range(NSTEP):
                    load_b(NSTEP * i + s, 2 * i + s // NS, s // NS, s % NS, s if first else RING,
                           last=(not before and s == NSTEP - 1))
                    if not (first and s < CLAG):
                        load_c(NSTEP * i + s - CLAG, (s - CLAG) // NS % 2, (s - CLAG) % NS, s - CLAG if first else RING)
                    for piece in SP_SIDE.get(s, "").split():
                        if (piece in AFTER and not after) or (piece in NEXT and not before):
                            continue
                        if piece == "x_in":
                            sp.wait_ge(xn_done, TT * (i + 1))
                            load_x_in(i + 1)
                        elif piece == "store":
                            if ends:
                                store(i - 2)
                        elif piece == "x1":
                            load_x1(i - 1)
                        elif piece == "rowsB":
                            store_rows(2 * i + 1, 1)
                        else:
                            store_rows(2 * i + 2, 0)

            load_x_in(0)
            sp.dma_start(modpack_sb, modpack).then_inc(modpack_loaded, 16)
            sp.dma_start(wt[:, 0:EARLY], wpack[:, 0:EARLY]).then_inc(w_early, 16)
            sp.dma_start(wt[:, EARLY:NW], wpack[:, EARLY:NW]).then_inc(w_late, 16)
            store_rows(0, 0)
            sp.wait_ge(rows_stored, 16)
            iteration(0, first=True, after=False, ends=False)
            iteration(1, ends=False)
            with sp.Fori(2, NCH - 1) as i:
                iteration(i)
            iteration(NCH - 1, before=False)
            for s in range(NS - CLAG, NS):
                load_c(NSTEP * (NCH - 1) + NS + s, 1, s, RING)
            store(NCH - 2)
            load_x1(NCH - 1)
            store(NCH - 1)
            sp.wait_ge(stored, 16 * NCH)
            sp.wait_ge(rows_stored, 16 * 2 * NCH)

        @block.tensor
        def _(pe):
            def transpose_tiles(dst, src):
                for s in range(TT):
                    last = nc.tensor.transpose(dst[:, s * P:(s + 1) * P], src[:, s * P:(s + 1) * P], ident)
                return last

            def ln1T(c):
                pe.wait_ge(xn_done, TT * (c + 1))
                transpose_tiles(ps_h1, xn[:].rearrange("p s d -> p (s d)")).then_inc(ln1_full, 1)

            def xi(q, d, k, c):
                pe.wait_ge(hT_done, CB * (c + 1))
                nc.tensor.matmul(pair[k][:], inw[:, d, k * P:(k + 1) * P], hT[:], start=True, stop=True).then_inc(xi_full, 1)

            def zz(q, d, k, c):
                pe.wait_ge(hT_done, CB * (c + 1))
                nc.tensor.matmul(h_pair[k][:], inw[:, d, DI + k * P:DI + (k + 1) * P], hT[:],
                                 start=True, stop=True).then_inc(z_full, 1)

            def xd(q, d):
                pe.wait_ge(u_done, q + 1)
                for k in range(ND):
                    last = nc.tensor.matmul(ps_h[0:XR, :], xpw[:, d, k, :], u[:, d, k, :], start=(k == 0), stop=(k == ND - 1))
                last.then_inc(xd_full, 1)

            def dt(q, d, k):
                pe.wait_ge(xdbl_done, q + 1)
                nc.tensor.matmul(pair[k][:], dtw[32:32 + DTR, d, k * P:(k + 1) * P], xdbl[32:32 + DTR, :],
                                 start=True, stop=True).then_inc(dt_full, 1)

            def nsum(t, q, n, first=False):
                pe.wait_ge(hc_done, t + 1)
                if n == 0 and not first:
                    pe.wait_ge(y_read, ND * q)
                for k in range(ND):
                    last = nc.tensor.matmul(ps_y[k][:], ident, hc[:, n % HB, k, :], start=(n == 0), stop=(n == NS - 1))
                last.then_inc(summed, 1)

            def outproj(c):
                for j in range(2 * ND):
                    d, k = j // ND, j % ND
                    if k == 0:
                        pe.wait_ge(y2_done, 2 * c + d + 1)
                    last = nc.tensor.matmul(stage[:], outw[:, d, k, :], y2[:, d, k, :], start=(j == 0), stop=(j == 2 * ND - 1))
                last.then_inc(out_full, 1)

            def attT(c):
                pe.wait_ge(att_done, CB * (c + 1))
                transpose_tiles(stage2, att).then_inc(attT_full, 1)

            def ln2T(c):
                pe.wait_ge(xn2_done, TT * (c + 1))
                transpose_tiles(ps_h, xn2[:].rearrange("p s d -> p (s d)")).then_inc(ln2_full, 1)

            def router(c):
                pe.wait_ge(h2T_done, CB * (c + 1))
                if not (isinstance(c, int) and c == 0):
                    pe.wait_ge(comb_s, NE * TT * c)
                for s in range(TT):
                    last = nc.tensor.matmul(ps_o[0][:, s * NE:(s + 1) * NE], h2T[:, s * P:(s + 1) * P], rw,
                                            start=True, stop=True)
                last.then_inc(router_full, 1)

            def hidden0(c, e):
                nc.tensor.matmul(ps_h[:], w1[:, e, 0:P], h2T[:], start=True, stop=True).then_inc(h_full, 1)

            def hidden1(c, e):
                nc.tensor.matmul(ps_h1[:], w1[:, e, P:2 * P], h2T[:], start=True, stop=True).then_inc(h_full, 1)

            def expert_out(c, e, first=False, last=False):
                if last:
                    pe.wait_ge(hidden_copied, 2 * NE * c + 2 * (e + 1))
                else:
                    pe.wait_ge(gelu_done, NE * c + e + 1)
                if e == 0:
                    pe.wait_ge(logits_done, c + 1)
                if not first:
                    pe.wait_ge(comb_s, NE * TT * c + TT * (e - 1))
                for s in range(TT):
                    for k in range(KF):
                        mm = nc.tensor.matmul(ps_o[e % 2][:, s * DM:(s + 1) * DM], g[:, e % GB, k, s * P:(s + 1) * P],
                                                w2[:, e, k, :], start=(k == 0), stop=(k == KF - 1))
                mm.then_inc(o_full, 1)

            def side(use, i, skip, before):
                c = i - 1
                if use.startswith("eo"):
                    e = int(use[2:])
                    expert_out(c, e, first=(e < 2 and isinstance(i, int) and i == 1))
                    return
                if use.startswith("xd"):
                    wait_bank(pe, "ps_h", use, i, skip, before)
                    xd(2 * i + (1 if use == "xdB" else 2), 1 if use == "xdB" else 0)
                    return
                if use.startswith("ffn"):
                    wait_bank(pe, "ps_h", use, i, skip, before)
                    hidden0(c, int(use[3:]))
                if use.startswith("ffn"):
                    wait_bank(pe, "ps_h1", use, i, skip, before)
                    hidden1(c, int(use[3:]))
                    return
                if use == "router":
                    router(c)
                    return
                wait_bank(pe, [bank for bank in BANK_USES if use in BANK_USES[bank]][0], use, i, skip, before)
                if use == "out":
                    outproj(c)
                elif use == "attT":
                    attT(c)
                elif use == "ln2T":
                    ln2T(c)
                elif use == "ln1T":
                    ln1T(i + 1)
                else:
                    back = "B" in use
                    d, q, cc = (1, 2 * i + 1, i) if back else (0, 2 * i + 2, i + 1)
                    k = int(use[-1])
                    if use.startswith("xi"):
                        xi(q, d, k, cc)
                    elif use.startswith("z"):
                        zz(q, d, k, cc)
                    else:
                        dt(q, d, k)

            def iteration(i, before, skip=(), first=False):
                q0 = 2 * i
                for s in range(NSTEP):
                    t = NSTEP * i + s
                    if s > 0:
                        nsum(t - 1, q0 + (s - 1) // NS, (s - 1) % NS, first=(first and s == 1))
                    elif not first:
                        nsum(t - 1, q0 - 1, NS - 1)
                    if first and s >= GATE_STEP and s < GATE_STEP + BATCH // 4:
                        gate_rows(s - GATE_STEP)
                    for use in PE_SIDE.get(s, "").split():
                        if use not in skip:
                            side(use, i, skip, before)

            def gate_rows(r):
                pe.wait_ge(mods_s, MODS)
                if r >= 2:
                    pe.wait_ge(gb_s, r - 1)
                for j in range(4):
                    b = 4 * r + j
                    last = nc.tensor.matmul(ps_o[r % 2][:, j * DM:(j + 1) * DM], mods[:, 5, b:b + 1].to_broadcast([P, P]),
                                            ident, start=True, stop=True)
                last.then_inc(gb_full, 1)

            pe.wait_ge(silu_c_done, 1)
            for j in range(6):
                last = nc.tensor.matmul(stage[:, j * BATCH:(j + 1) * BATCH],
                                        wmod[:, j * DM:(j + 1) * DM], silu_c[:], start=True, stop=True)
            last.then_inc(mod_full, 1)
            pe.wait_ge(w_early, 16)
            pe.wait_ge(mods_s, 1)
            for use in [x for x in PE_ORDER if x in NEXT]:
                side(use, -1, [x for x in EVERY_USE if x not in NEXT],
                     {"stage": (mods_s, 1), "stage2": (mods_s, 1), "ps_h": None, "ps_h1": None})
            pe.wait_ge(w_late, 16)

            def last_uses(i, skip=()):
                kept = {bank: [x for x in uses if x not in skip] for bank, uses in BANK_USES.items()}
                return {bank: reader(bank, uses[-1], i) if uses else None for bank, uses in kept.items()}

            iteration(0, last_uses(-1, AFTER), skip=AFTER, first=True)
            pe.wait_ge(gb_s, BATCH // 4)
            iteration(1, last_uses(0, AFTER))
            with pe.Fori(2, NCH - 1) as i:
                iteration(i, last_uses(i - 1))
            iteration(NCH - 1, last_uses(NCH - 2), skip=NEXT)
            nsum(NSTEP * NCH - 1, 2 * NCH - 1, NS - 1)

            def tail(use):
                side(use, NCH, [x for x in EVERY_USE if x not in AFTER], last_uses(NCH - 1, NEXT))

            for use in ("out", "attT", "ln2T", "router", "ffn0"):
                tail(use)
            for e in range(NE):
                if e + 1 < NE:
                    tail(f"ffn{e + 1}")
                expert_out(NCH - 1, e, last=True)

        @block.scalar
        def _(act):
            def xn1(c):
                act.wait_ge(ln1_s, NORM * (c + 1))
                for s in range(TT):
                    nc.scalar.activation(xn[:, s, :], x_in[:, s, :], ACT.Identity, scale=rstd[:, s:s + 1],
                                         bias=shift[:, s:s + 1]).then_inc(xn_done, 1)

            def modulate1(c):
                act.wait_ge(ln1_full, c + 1)
                for b in range(CB):
                    nc.scalar.activation(hT[:, b * SEQ:(b + 1) * SEQ], ps_h1[:, b * SEQ:(b + 1) * SEQ], ACT.Identity,
                                         scale=mods[:, 1, bass.ds(CB * c + b, 1)],
                                         bias=mods[:, 0, bass.ds(CB * c + b, 1)]).then_inc(hT_done, 1)

            def centre(q, d, k):
                act.wait_ge(xi_full, ND * q + k + 1)
                if k == 0 and not (isinstance(q, int) and q == 0):
                    act.wait_ge(expln_s, 3 * q)
                    act.wait_ge(corr_done, q)
                nc.scalar.activation(xc[:, k, :], pair[k][:], ACT.Identity, scale=convw[:, d, k, TAPS - 1:TAPS],
                                     bias=convb[:, d, k:k + 1]).then_inc(centre_done, 1)

            def silus(q, d):
                for k in range(ND):
                    act.wait_ge(z_full, ND * q + k + 1)
                    if k == 0 and not (isinstance(q, int) and q < 2):
                        act.wait_ge(y2_done, q - 1)
                    nc.scalar.activation(sz[:, d, k, :], h_pair[k][:], ACT.Silu).then_inc(sz_done, 1)
                act.wait_ge(conv_s, ND * (TAPS - 1) * (q + 1))
                if not (isinstance(q, int) and q < 2):
                    act.wait_ge(y_read, ND * (q - 1))
                nc.scalar.activation(u[:, d], xc[:], ACT.Silu).then_inc(u_done, 1)

            def xdbl_copy(q, d):
                act.wait_ge(xd_full, q + 1)
                if not (isinstance(q, int) and q == 0):
                    act.wait_ge(rows_stored, 16 * q)
                nc.scalar.copy(xdbl[0:XR, :], ps_h[0:XR, :]).then_inc(xdbl_done, 1)

            def dt_acts(q, d, k, first=False):
                act.wait_ge(dt_full, ND * q + k + 1)
                if k == 0 and not first:
                    act.wait_ge(delta_s, DPARTS * (q - 1) + 2)
                nc.scalar.activation(sp_e[:, k, :], pair[k][:], ACT.Abs, bias=dtb[:, d, k:k + 1]).then_inc(dt_act, 1)
                nc.scalar.activation(sp_r[:, k, :], pair[k][:], ACT.Relu, bias=dtb[:, d, k:k + 1]).then_inc(dt_act, 1)

            def exp_ln(q):
                act.wait_ge(dt_act, 2 * ND * (q + 1))
                nc.scalar.activation(sp_e[:], sp_e[:], ACT.Exp, scale=-1.0).then_inc(expln_s, 1)
                act.wait_ge(expln_s, 3 * q + 1)
                nc.scalar.activation(xc[:], sp_e[:], ACT.Identity, bias=1.0).then_inc(expln_s, 1)
                act.wait_ge(expln_s, 3 * q + 2)
                nc.scalar.activation(sp_l[:], xc[:], ACT.Ln).then_inc(expln_s, 1)

            def step(t, q, d, n, head):
                r = n % RING
                if n == 0:
                    act.wait_ge(delta_s, DPARTS * q + 2)
                if head >= RING:
                    act.wait_ge(scan_done, t - RING + 1)
                else:
                    act.wait_ge(zeroed, 1)
                for k in range(ND):
                    nc.scalar.activation(seqs(decay, r)[:, k], delta[:, d, k, :].rearrange("p (b t) -> p b t", b=CB),
                                         ACT.Exp, scale=amat[:, d, k, n:n + 1]).then_inc(decay_done, 1)

            def att_scale(c):
                act.wait_ge(out_full, c + 1)
                for b in range(CB):
                    nc.scalar.activation(att[:, b * SEQ:(b + 1) * SEQ], stage[:, b * SEQ:(b + 1) * SEQ], ACT.Identity,
                                         scale=mods[:, 2, bass.ds(CB * c + b, 1)]).then_inc(att_done, 1)

            def xn2_(c):
                act.wait_ge(ln2_s, NORM * (c + 1))
                for s in range(TT):
                    nc.scalar.activation(xn2[:, s, :], x1[:, s, :], ACT.Identity, scale=rstd2[:, s:s + 1],
                                         bias=shift2[:, s:s + 1]).then_inc(xn2_done, 1)

            def modulate2(c):
                act.wait_ge(ln2_full, c + 1)
                for b in range(CB):
                    nc.scalar.activation(h2T[:, b * SEQ:(b + 1) * SEQ], ps_h[:, b * SEQ:(b + 1) * SEQ], ACT.Identity,
                                         scale=mods[:, 4, bass.ds(CB * c + b, 1)],
                                         bias=mods[:, 3, bass.ds(CB * c + b, 1)]).then_inc(h2T_done, 1)

            def gate_exp(c):
                act.wait_ge(gap_done, c + 1)
                nc.scalar.activation(gap_e[:], gap[:], ACT.Exp).then_inc(gap_exp, 1)

            def hidden_copy(c, e, head=False):
                for k in range(KF):
                    act.wait_ge(h_full, 2 * NE * c + 2 * e + k + 1)
                    if k == 0 and not (head and e < GB):
                        act.wait_ge(o_full, NE * c + max(0, e - GB + 1))
                    nc.scalar.copy(g[:, e % GB, k, :], (ps_h if k == 0 else ps_h1)[:]).then_inc(hidden_copied, 1)

            def hidden_gelu(c, e):
                for k in range(KF):
                    act.wait_ge(h_full, 2 * NE * c + 2 * e + k + 1)
                    if k == 0:
                        act.wait_ge(o_full, NE * c + max(0, e - GB + 1))
                    nc.scalar.activation(g[:, e % GB, k, :], h_pair[k][:], ACT.Gelu).then_inc(hidden_copied, 1)

            def gelus(c, e0):
                act.wait_ge(hidden_copied, 2 * NE * c + 2 * (e0 + GS))
                for e in range(e0, e0 + GS):
                    nc.scalar.activation(g[:, e % GB], g[:, e % GB], ACT.Gelu).then_inc(gelu_done, 1)

            def side(s, i, after=True, before=True, first=False, second=False):
                c = i - 1
                for piece in ACT_SIDE.get(s, "").split():
                    if (piece in AFTER and not after) or (piece in NEXT and not before):
                        continue
                    q, d, cc = (2 * i + 1, 1, i) if "B" in piece else (2 * i + 2, 0, i + 1)
                    if piece.startswith("centre"):
                        centre(q, d, int(piece[-1]))
                    elif piece.startswith("silu"):
                        silus(q, d)
                    elif piece.startswith("xd"):
                        xdbl_copy(q, d)
                    elif piece.startswith("dt"):
                        dt_acts(q, d, int(piece[-1]))
                    elif piece.startswith("expln"):
                        exp_ln(q)
                    elif piece == "xn1":
                        xn1(i + 1)
                    elif piece == "mod1":
                        modulate1(i + 1)
                    elif piece == "att":
                        att_scale(c)
                    elif piece == "xn2":
                        xn2_(c)
                    elif piece == "mod2":
                        modulate2(c)
                    elif piece == "gapexp":
                        gate_exp(c)
                    elif piece.startswith("hid"):
                        hidden_copy(c, int(piece[3:]), second)
                    else:
                        gelus(c, GS * int(piece[4:]))

            def iteration(i, first=False, **kw):
                for s in range(NSTEP):
                    step(NSTEP * i + s, 2 * i + s // NS, s // NS, s % NS, s if first else RING)
                    side(s - LEAD, i, first=first, **kw)
                    r = s - LEAD - GATE_STEP - 2
                    if first and 0 <= r < BATCH // 4:
                        act.wait_ge(gb_full, r + 1)
                        nc.scalar.copy(gb_rows[:, 4 * r:4 * r + 4, :].rearrange("p b d -> p (b d)"),
                                       ps_o[r % 2][:]).then_inc(gb_s, 1)

            act.wait_ge(modpack_loaded, 16)
            nc.scalar.activation(silu_c[:], ct, ACT.Silu).then_inc(silu_c_done, 1)
            xn1(0)
            act.wait_ge(mod_full, 1)
            nc.scalar.copy(mods[:].rearrange("p j b -> p (j b)"), stage[:, 0:6 * BATCH]).then_inc(mods_s, 1)
            act.wait_ge(w_early, 16)
            act.wait_ge(mods_s, MODS)
            modulate1(0)
            centre(0, 0, 0)
            centre(0, 0, 1)
            silus(0, 0)
            nc.scalar.activation(amat[:].rearrange("p r k n -> p (r k n)"), field("alog"), ACT.Exp).then_inc(a_exp, 1)
            xdbl_copy(0, 0)
            dt_acts(0, 0, 0, True)
            dt_acts(0, 0, 1)
            exp_ln(0)
            act.wait_ge(a_neg, 1)
            iteration(0, first=True, after=False)
            iteration(1, second=True)
            with act.Fori(2, NCH - 1) as i:
                iteration(i)
            iteration(NCH - 1, before=False)
            c = NCH - 1
            att_scale(c)
            xn2_(c)
            modulate2(c)
            gate_exp(c)
            for e in range(NE):
                hidden_gelu(c, e)

        @block.vector
        def _(dve):
            def norm_stats(src, st, m, v, s_, hold, c):
                for s in range(TT):
                    nc.vector.bn_stats(st[:, s, :], src[:, s, :]).then_inc(s_, 1)
                dve.wait_ge(s_, NORM * c + TT)
                nc.vector.memset(held[0:1, hold:hold + 1], 0.0)
                for s in range(TT):
                    nc.vector.bn_aggr(m[:, s, :], st[:, s, :]).then_inc(s_, 1)
                dve.wait_ge(s_, NORM * c + 2 * TT)
                nc.vector.tensor_scalar(v[:], m[:, :, 1], EPS, None, ALU.add).then_inc(s_, 1)

            def norm_root(m, v, rs, tmp, sh, s_, seed_done, c):
                n0 = NORM * c + 2 * TT + 1
                dve.wait_ge(seed_done, c + 1)
                nc.vector.scalar_tensor_tensor(out=tmp[:], in0=rs[:], scalar=-0.5, in1=rs[:], op0=ALU.mult,
                                               op1=ALU.mult).then_inc(s_, 1)
                dve.wait_ge(s_, n0 + 1)
                nc.vector.tensor_tensor(tmp[:], tmp[:], v[:], ALU.mult).then_inc(s_, 1)
                dve.wait_ge(s_, n0 + 2)
                nc.vector.scalar_tensor_tensor(out=rs[:], in0=tmp[:], scalar=1.5, in1=rs[:], op0=ALU.add,
                                               op1=ALU.mult).then_inc(s_, 1)
                dve.wait_ge(s_, n0 + 3)
                nc.vector.scalar_tensor_tensor(out=sh[:], in0=m[:, :, 0], scalar=-1.0, in1=rs[:], op0=ALU.mult,
                                               op1=ALU.mult).then_inc(s_, 1)

            def ln1(c, first=False):
                dve.wait_ge(x_in_loaded, 16 * (c + 1))
                if not first:
                    dve.wait_ge(xn_done, TT * c)
                norm_stats(x_in, stats, mv, var, ln1_s, 0, c)

            def ln1_root(c):
                norm_root(mv, var, rstd, newton, shift, ln1_s, seed1, c)

            def tap(q, d, j):
                shift_by = TAPS - 1 - j
                there, here = slice(0, SEQ - shift_by), slice(shift_by, SEQ)
                if d:
                    there, here = here, there
                for k in range(ND):
                    v = xc[:, k, :].rearrange("p (b t) -> p b t", b=CB)
                    x = pair[k][:].rearrange("p (b t) -> p b t", b=CB)
                    if j == 0:
                        dve.wait_ge(centre_done, ND * q + k + 1)
                    else:
                        dve.wait_ge(conv_s, ND * ((TAPS - 1) * q + j - 1) + k + 1)
                    nc.vector.scalar_tensor_tensor(out=v[:, :, here], in0=x[:, :, there],
                                                   scalar=convw[:, d, k, j:j + 1], in1=v[:, :, here], op0=ALU.mult,
                                                   op1=ALU.add).then_inc(conv_s, 1)

            def correction(q):
                dve.wait_ge(expln_s, 3 * q + 2)
                nc.vector.scalar_tensor_tensor(out=sp_e[:], in0=xc[:], scalar=-1.0, in1=sp_e[:], op0=ALU.add,
                                               op1=ALU.subtract).then_inc(corr_done, 1)

            def scan(t, q, d, n, head):
                r = n % RING
                dve.wait_ge(decay_done, ND * (t + 1))
                dve.wait_ge(drive_done, t + 1)
                if head >= SB:
                    dve.wait_ge(hc_done, t - SB + 1)
                rng = slice(None, None, -1) if d else slice(None)
                nc.vector.tensor_tensor_scan(state[:, n % SB, 0:WP - 1][:, rng], decay[:, r, 0:WP - 1][:, rng],
                                             drive[:, r, 0:WP - 1][:, rng], 0.0, ALU.mult, ALU.add).then_inc(scan_done, 1)

            def times_c(t, q, n, head):
                dve.wait_ge(scan_done, t + 1)
                dve.wait_ge(c_loaded[n % CRING], 16 * (NS // CRING * q + n // CRING + 1))
                if head >= HB:
                    dve.wait_ge(summed, t - HB + 1)
                nc.vector.tensor_tensor(hc[:, n % HB].rearrange("p k (b t) -> p k b t", b=CB), seqs(state, n % SB),
                                        c_sb[:, n % CRING, :].rearrange("p (b t) -> p b t", b=CB).unsqueeze(1)
                                        .to_broadcast([P, ND, CB, SEQ]), ALU.mult).then_inc(hc_done, 1)

            def residual(c):
                dve.wait_ge(attT_full, c + 1)
                dve.wait_ge(x1_loaded, 16 * (c + 1))
                nc.vector.tensor_tensor(x1[:].rearrange("p s d -> p (s d)"), stage2[:],
                                        x1[:].rearrange("p s d -> p (s d)"), ALU.add).then_inc(x1_done, 1)

            def ln2(c):
                dve.wait_ge(x1_done, c + 1)
                norm_stats(x1, stats2, mv2, var2, ln2_s, 1, c)

            def ln2_root(c):
                norm_root(mv2, var2, rstd2, newton2, shift2, ln2_s, seed2, c)

            def route_a(c):
                dve.wait_ge(router_full, c + 1)
                nc.vector.tensor_copy(logits[:].rearrange("p s e -> p (s e)"), ps_o[0][:, 0:TT * NE]).then_inc(logits_done, 1)
                dve.wait_ge(logits_done, c + 1)
                nc.vector.memset(held[0:1, 2:3], 0.0)
                n0 = 2 * TT + 7
                for s in range(TT):
                    nc.vector.max(top[:, s, :], logits[:, s, :]).then_inc(route_s, 1)
                dve.wait_ge(route_s, n0 * c + TT)
                nc.vector.memset(held[0:1, 3:4], 0.0)
                for s in range(TT):
                    nc.vector.max_index(top_i[:, s, :], top[:, s, :], logits[:, s, :]).then_inc(route_s, 1)
                nc.vector.tensor_tensor(gap[:], top[:, :, 1:2], top[:, :, 0:1], ALU.subtract).then_inc(gap_done, 1)
                dve.wait_ge(route_s, n0 * c + 2 * TT)
                nc.vector.tensor_copy(top_f[:], top_i[:, :, 0:2]).then_inc(route_s, 1)

            def route_b(c):
                n0 = 2 * TT + 7
                k0 = n0 * c + 2 * TT + 1
                dve.wait_ge(gap_exp, c + 1)
                nc.vector.tensor_scalar(gate[:, :, 0:1], gap_e[:], 1.0, None, ALU.add).then_inc(route_s, 1)
                dve.wait_ge(route_s, k0 + 1)
                nc.vector.reciprocal(gate[:, :, 1:2], gate[:, :, 0:1]).then_inc(route_s, 1)
                dve.wait_ge(route_s, k0 + 2)
                nc.vector.tensor_tensor(gate[:, :, 2:3], gate[:, :, 1:2], gap_e[:], ALU.mult).then_inc(route_s, 1)
                for j in range(2):
                    nc.vector.tensor_tensor(pick[:, j], iota8.unsqueeze(1).to_broadcast([P, TT, NE]),
                                            top_f[:, :, j:j + 1].to_broadcast([P, TT, NE]), ALU.is_equal).then_inc(route_s, 1)
                dve.wait_ge(route_s, k0 + 5)
                nc.vector.tensor_tensor(pick[:].rearrange("p j s e -> p s j e"), pick[:].rearrange("p j s e -> p s j e"),
                                        gate[:, :, 1:3].unsqueeze(3).to_broadcast([P, TT, 2, NE]),
                                        ALU.mult).then_inc(route_s, 1)
                dve.wait_ge(route_s, k0 + 6)
                nc.vector.tensor_tensor(wexp[:], pick[:, 0], pick[:, 1], ALU.add).then_inc(wexp_done, 1)

            def combine(c, e):
                dve.wait_ge(o_full, NE * c + e + 1)
                if e == 0:
                    dve.wait_ge(wexp_done, c + 1)
                    if not (isinstance(c, int) and c == 0):
                        dve.wait_ge(stored, 16 * c)
                else:
                    dve.wait_ge(comb_s, NE * TT * c + TT * e)
                for s in range(TT):
                    src = ps_o[e % 2][:, s * DM:(s + 1) * DM]
                    if e == 0:
                        nc.vector.tensor_scalar(acc[:, s, :], src, wexp[:, s, 0:1], None, ALU.mult).then_inc(comb_s, 1)
                    else:
                        nc.vector.scalar_tensor_tensor(out=acc[:, s, :], in0=src, scalar=wexp[:, s, e:e + 1],
                                                       in1=acc[:, s, :], op0=ALU.mult, op1=ALU.add).then_inc(comb_s, 1)

            def side(s, i, after=True, before=True, first=False, last=False):
                c = i - 1
                for piece in DVE_SIDE.get(s, "").split():
                    if (piece in AFTER and not after) or (piece in NEXT and not before) or (last and piece not in AFTER):
                        continue
                    q, d = (2 * i + 1, 1) if "B" in piece else (2 * i + 2, 0)
                    if piece == "ln1":
                        ln1(i + 1)
                    elif piece == "root1":
                        ln1_root(i + 1)
                    elif piece.startswith("tap"):
                        tap(q, d, int(piece[-1]))
                    elif piece.startswith("corr"):
                        correction(q)
                    elif piece == "yB":
                        y_out_b(c)
                    elif piece == "yF":
                        y_out_f(i)
                    elif piece == "res":
                        residual(c)
                        ln2(c)
                    elif piece == "root2":
                        ln2_root(c)
                    elif piece == "routeA":
                        route_a(c)
                    elif piece == "routeB":
                        route_b(c)
                    else:
                        combine(c, int(piece[4:]))

            def y_out_b(c):
                y_pass(2 * c + 1, 1, c)

            def y_out_f(c):
                y_pass(2 * c, 0, c)

            def y_pass(q, d, c):
                dve.wait_ge(summed, NS * (q + 1))
                if not (isinstance(c, int) and c == 0):
                    dve.wait_ge(out_full, c)
                for k in range(ND):
                    nc.vector.scalar_tensor_tensor(out=y2[:, d, k, :], in0=u[:, d, k, :], scalar=dp[:, d, k:k + 1],
                                                   in1=ps_y[k][:], op0=ALU.mult, op1=ALU.add).then_inc(y_read, 1)

            def iteration(i, first=False, **kw):
                for s in range(NSTEP):
                    t = NSTEP * i + s
                    scan(t, 2 * i + s // NS, s // NS, s % NS, s if first else RING)
                    if not (first and s == 0):
                        times_c(t - 1, 2 * i + (s - 1) // NS, (s - 1) % NS, s - 1 if first else RING)
                    side(s, i, first=first, **kw)

            def delta_part_0(part):
                if part == 0:
                    dve.wait_ge(dt_act, 2 * ND)
                    dve.wait_ge(corr_done, 1)
                    nc.vector.tensor_tensor(sp_r[:], sp_r[:], sp_e[:], ALU.subtract).then_inc(delta_s, 1)
                elif part == 1:
                    dve.wait_ge(expln_s, 3)
                    dve.wait_ge(delta_s, 1)
                    nc.vector.tensor_tensor(delta[:, 0], sp_l[:], sp_r[:], ALU.add).then_inc(delta_s, 1)
                else:
                    dve.wait_ge(delta_s, 2)
                    nc.vector.tensor_tensor(du[:, 0], delta[:, 0], u[:, 0], ALU.mult).then_inc(delta_s, 1)

            ln1(0, first=True)
            ln1_root(0)
            dve.wait_ge(mods_s, 1)
            nc.vector.tensor_scalar(mods[:, 1], mods[:, 1], 1.0, None, ALU.add).then_inc(mods_s, 1)
            nc.vector.tensor_scalar(mods[:, 4], mods[:, 4], 1.0, None, ALU.add).then_inc(mods_s, 1)
            gates = mods[:].rearrange("p (h j) b -> p h j b", h=2)[:, :, 2, :]
            nc.vector.scalar_tensor_tensor(out=mod_t[:, 0], in0=gates, scalar=-1.0, in1=gates, op0=ALU.mult,
                                           op1=ALU.max).then_inc(mods_s, 1)
            nc.vector.tensor_scalar(mod_t[:, 1], gates, 0.0, 0.5, ALU.is_ge, ALU.subtract).then_inc(mods_s, 1)
            dve.wait_ge(mods_s, 5)
            nc.vector.scalar_tensor_tensor(out=gates, in0=mod_t[:, 0], scalar=0.25, in1=mod_t[:, 1], op0=ALU.max,
                                           op1=ALU.mult).then_inc(mods_s, 1)
            dve.wait_ge(mods_s, 6)
            nc.vector.tensor_scalar(mods[:, 5], mods[:, 5], 2.0, None, ALU.mult).then_inc(mods_s, 1)
            nc.vector.memset(decay[:].rearrange("p r (k t) -> p r k t", t=PAD)[:, :, :, SEQ:PAD], 0.0)
            nc.vector.memset(drive[:].rearrange("p r (k t) -> p r k t", t=PAD)[:, :, :, SEQ:PAD], 0.0).then_inc(zeroed, 1)
            for j in range(TAPS - 1):
                tap(0, 0, j)
            dve.wait_ge(a_exp, 1)
            nc.vector.tensor_scalar(amat[:].rearrange("p r k n -> p (r k n)"),
                                    amat[:].rearrange("p r k n -> p (r k n)"), -1.0, None, ALU.mult).then_inc(a_neg, 1)
            correction(0)
            for part in range(DPARTS):
                delta_part_0(part)
            iteration(0, first=True, after=False)
            iteration(1)
            with dve.Fori(2, NCH - 1) as i:
                iteration(i)
            iteration(NCH - 1, before=False)
            times_c(NSTEP * NCH - 1, 2 * NCH - 1, NS - 1, RING)
            for s in range(NSTEP):
                side(s, NCH, before=False, last=True)
                if DVE_SIDE.get(s) == "yB":
                    dve.wait_ge(y_read, ND * 2 * NCH)
                    nc.vector.tensor_tensor(y2[:, 1], y2[:, 1], sz[:, 1], ALU.mult).then_inc(y2_done, 1)
            c = NCH - 1
            dve.wait_ge(comb_s, NE * TT * NCH)
            rows = acc[:].rearrange("p (b s) d -> p b s d", b=CB)
            nc.vector.tensor_tensor(rows, rows, gb_rows[:, CB * c:CB * c + CB, :].unsqueeze(2)
                                    .to_broadcast([P, CB, TT // CB, DM]), ALU.mult).then_inc(out_s, 1)
            dve.wait_ge(out_s, 2 * c + 1)
            nc.vector.tensor_tensor(acc[:], acc[:], x1[:], ALU.add).then_inc(out_s, 1)

        @block.gpsimd
        def _(pool):
            def root_seed(v, rs, s_, seed_done, used, c):
                pool.wait_ge(s_, NORM * c + 2 * TT + 1)
                if not (isinstance(c, int) and c == 0):
                    pool.wait_ge(used, TT * c)
                nc.gpsimd.tensor_tensor(rs[:], v[:], minus_half[:], ALU.pow).then_inc(seed_done, 1)

            def delta_part(q, d, part):
                if part == 0:
                    pool.wait_ge(dt_act, 2 * ND * (q + 1))
                    pool.wait_ge(corr_done, q + 1)
                    nc.gpsimd.tensor_tensor(sp_r[:], sp_r[:], sp_e[:], ALU.subtract).then_inc(delta_s, 1)
                elif part == 1:
                    pool.wait_ge(expln_s, 3 * (q + 1))
                    pool.wait_ge(delta_s, DPARTS * q + 1)
                    nc.gpsimd.tensor_tensor(delta[:, d], sp_l[:], sp_r[:], ALU.add).then_inc(delta_s, 1)
                else:
                    pool.wait_ge(delta_s, DPARTS * q + 2)
                    nc.gpsimd.tensor_tensor(du[:, d], delta[:, d], u[:, d], ALU.mult).then_inc(delta_s, 1)

            def drive_step(t, q, d, n, head):
                r = n % RING
                pool.wait_ge(b_loaded[r], 16 * (NS // RING * q + n // RING + 1))
                if n == 0:
                    pool.wait_ge(delta_s, DPARTS * (q + 1))
                if head >= RING:
                    pool.wait_ge(scan_done, t - RING + 1)
                else:
                    pool.wait_ge(zeroed, 1)
                nc.gpsimd.tensor_tensor(seqs(drive, r), du[:, d].rearrange("p k (b t) -> p k b t", b=CB),
                                        b_sb[:, r, :].rearrange("p (b t) -> p b t", b=CB).unsqueeze(1)
                                        .to_broadcast([P, ND, CB, SEQ]), ALU.mult).then_inc(drive_done, 1)

            def gate_y(q, d):
                pool.wait_ge(y_read, ND * (q + 1))
                nc.gpsimd.tensor_tensor(y2[:, d], y2[:, d], sz[:, d], ALU.mult).then_inc(y2_done, 1)

            def finish(c):
                pool.wait_ge(comb_s, NE * TT * (c + 1))
                rows = acc[:].rearrange("p (b s) d -> p b s d", b=CB)
                nc.gpsimd.tensor_tensor(rows, rows, gb_rows[:, bass.ds(CB * c, CB), :].unsqueeze(2)
                                        .to_broadcast([P, CB, TT // CB, DM]), ALU.mult).then_inc(out_s, 1)
                pool.wait_ge(out_s, 2 * c + 1)
                nc.gpsimd.tensor_tensor(acc[:], acc[:], x1[:], ALU.add).then_inc(out_s, 1)

            def iteration(i, first=False, after=True, before=True, ends=True):
                for s in range(NSTEP):
                    drive_step(NSTEP * i + s, 2 * i + s // NS, s // NS, s % NS, s if first else RING)
                    for piece in POOL_SIDE.get(s, "").split():
                        if (piece in AFTER and not after) or (piece in NEXT and not before):
                            continue
                        if piece == "finish":
                            if ends:
                                finish(i - 2)
                        elif piece == "gateB":
                            gate_y(2 * i - 1, 1)
                        elif piece == "gateF":
                            gate_y(2 * i, 0)
                        elif piece == "seed1":
                            root_seed(var, rstd, ln1_s, seed1, xn_done, i + 1)
                        elif piece == "seed2":
                            root_seed(var2, rstd2, ln2_s, seed2, xn2_done, i - 1)
                        elif piece.startswith("dB"):
                            delta_part(2 * i + 1, 1, int(piece[2:]))
                        else:
                            delta_part(2 * i + 2, 0, int(piece[2:]))

            nc.gpsimd.memset(minus_half[:], -0.5).then_inc(half_set, 1)
            pool.wait_ge(half_set, 1)
            root_seed(var, rstd, ln1_s, seed1, xn_done, 0)
            iteration(0, first=True, after=False, ends=False)
            iteration(1, ends=False)
            pool.wait_ge(gb_s, BATCH // 4)
            with pool.Fori(2, NCH - 1) as i:
                iteration(i)
            iteration(NCH - 1, before=False)
            finish(NCH - 2)
            root_seed(var2, rstd2, ln2_s, seed2, xn2_done, NCH - 1)


def kernel(**inputs):
    import numpy as np
    import concourse.bacc as bacc
    from concourse.bass_utils import run_bass_kernel_spmd as run

    a = {k: np.asarray(v) for k, v in inputs.items()}
    pack = np.zeros((P, NW), np.float32)

    def put(name, value):
        lo, hi = AT[name]
        pack[:, lo:hi] = value.reshape(P, hi - lo)

    def both(name):
        return [a[f"L0_attn_{name}_f"], a[f"L0_attn_{name}_b"]]

    def channels(v):
        return v.reshape(ND, P, -1).transpose(1, 0, 2)

    put("ident", np.eye(P, dtype=np.float32))
    put("iota8", np.tile(np.arange(NE, dtype=np.float32), (P, 1)))
    put("inw", np.stack([v.T for v in both("inW")], 1))
    xp = np.zeros((P, 2, ND, XR), np.float32)
    for d, v in enumerate(both("xpW")):
        cols = channels(v.T)
        xp[:, d, :, :2 * NS] = cols[:, :, DTR:]
        xp[:, d, :, 2 * NS:] = cols[:, :, :DTR]
    put("xpw", xp)
    dtw = np.zeros((P, 2, DI), np.float32)
    for d, v in enumerate(both("dtW")):
        dtw[32:32 + DTR, d] = v.T
    put("dtw", dtw)
    put("convw", np.stack([channels(v.reshape(DI, TAPS)) for v in both("convW")], 1))
    put("convb", np.stack([channels(v)[:, :, 0] for v in both("convB")], 1))
    put("dtb", np.stack([channels(v)[:, :, 0] for v in both("dtB")], 1))
    put("alog", np.stack([channels(v) for v in both("Alog")], 1))
    put("dp", np.stack([channels(v)[:, :, 0] for v in both("Dp")], 1))
    put("rw", a["L0_ffn_router_w"].T)
    put("outw", np.stack([channels(v.T) for v in both("outW")], 1))
    put("w1", a["L0_ffn_w1"].transpose(1, 0, 2))
    put("w2", a["L0_ffn_w2"].reshape(NE, KF, P, DM).transpose(2, 0, 1, 3))
    x_l = np.ascontiguousarray(a["L0_attn_x"].reshape(NCH, TT, P, DM).transpose(0, 2, 1, 3)).reshape(NCH, P, TT * DM)

    nc = bacc.Bacc("TRN2", target_bir_lowering=False, num_devices=1)
    arrays = {"x_l": x_l, "modpack": np.concatenate([a["L0_c"].T, a["L0_wmod"]], 1), "wpack": pack}
    args = [nc.dram_tensor(k, v.shape, mybir.dt.from_np(v.dtype), kind="ExternalInput").ap() for k, v in arrays.items()]
    args.append(nc.dram_tensor("bc_rows", (2, 2 * NS, CT), F32, kind="Internal").ap())
    args.append(nc.dram_tensor("out_l", x_l.shape, F32, kind="ExternalOutput").ap())
    build(nc, *args)
    r = run(nc, [arrays], core_ids=[0])
    return np.asarray(r.results[0]["out_l"]).reshape(NCH, P, TT, DM).transpose(0, 2, 1, 3).reshape(BATCH, SEQ, DM)
```
